# Optimizing a Trainium2 kernel written in Bass

```python
import numpy as np
import jax
import jax.numpy as jnp

def _softmax(x, axis=-1):
    return jax.nn.softmax(x, axis=axis)

def _gelu(x):
    return jax.nn.gelu(x, approximate=True)

def _silu(x):
    return jax.nn.silu(x)

def _sigmoid(x):
    return jax.nn.sigmoid(x)

def _layernorm(x, axis=-1, eps=1e-05):
    m = jnp.mean(x, axis=axis, keepdims=True)
    v = jnp.var(x, axis=axis, keepdims=True)
    return (x - m) / jnp.sqrt(v + eps)

def _scatter_add(tgt, idx, src, axis=0):
    return tgt.at[idx].add(src)

def _segment_sum(src, seg, n):
    return jax.ops.segment_sum(src, seg, n)
kernel_name = 'mk_xattn_seq_d2_seqx_r8_20038a'

def setup_inputs(seed: int=0):
    np.random.seed(seed)
    _w = jnp.asarray

    def _rec_inputs():
        import jax
        import jax.numpy as jnp
        _rk = jax.random.key(seed)
        x = 7.22e-05 + 1 * jax.random.normal(jax.random.fold_in(_rk, 1), (64, 64, 256), jnp.float32)
        _lenS = 64 - jax.random.randint(jax.random.fold_in(_rk, 7), (64,), 0, max(1, 64 // 4) + 1, jnp.int32)
        _lenS2 = 64 - jax.random.randint(jax.random.fold_in(_rk, 8), (64,), 0, max(1, 64 // 4) + 1, jnp.int32)
        _ctx_2048P = jax.random.normal(jax.random.fold_in(_rk, 11), (64, 16, 256), jnp.float32)
        _ctx_2048c = jax.random.dirichlet(jax.random.fold_in(_rk, 511), 0.3 * jnp.ones((16,), jnp.float32), (64, 64))
        _ctx_2048t = jnp.einsum('bsk,bkd->bsd', _ctx_2048c, _ctx_2048P)
        _ctx_2048t = _ctx_2048t * jax.lax.rsqrt(jnp.mean(jnp.square(_ctx_2048t)) + 1e-12) * 0.953939
        ctx_2048 = 4.13588e-05 + 0.999923 * (_ctx_2048t + 0.3 * jax.random.normal(jax.random.fold_in(_rk, 611), (64, 64, 256), jnp.float32))
        return (x, ctx_2048)
    x, ctx_2048 = _rec_inputs()

    def _L0_xattn_setup():
        import jax, jax.numpy as jnp
        import numpy as np
        B, C, CI, T = (8, 64, 32, 256)
        EPS = 1e-05
        key = jax.random.key(seed)
        ks = jax.random.split(key, 8)
        inv_c = 1.0 / np.sqrt(C)
        inv_ci = 1.0 / np.sqrt(CI)
        return {'x_this': jax.random.normal(ks[0], (B, C, T), jnp.float32), 'x_other': jax.random.normal(ks[1], (B, C, T), jnp.float32), 'Wg': jax.random.normal(ks[2], (CI, C), jnp.float32) * inv_c, 'bg': jnp.zeros((CI,), jnp.float32), 'Wtheta': jax.random.normal(ks[3], (CI, C), jnp.float32) * inv_c, 'btheta': jnp.zeros((CI,), jnp.float32), 'Wphi': jax.random.normal(ks[4], (CI, C), jnp.float32) * inv_c, 'bphi': jnp.zeros((CI,), jnp.float32), 'Wz': jax.random.normal(ks[5], (C, CI), jnp.float32) * inv_ci, 'bz': jnp.zeros((C,), jnp.float32), 'gamma': jax.random.normal(ks[6], (C,), jnp.float32), 'beta': jax.random.normal(ks[7], (C,), jnp.float32)}
    _L0_xattn_all = _L0_xattn_setup()
    _L0_xattn_in = {k: v for k, v in _L0_xattn_all.items() if k in ('Wg', 'bg', 'Wtheta', 'btheta', 'Wphi', 'bphi', 'Wz', 'bz', 'gamma', 'beta')}
    del _L0_xattn_all

    def _L1_xattn_setup():
        import jax, jax.numpy as jnp
        import numpy as np
        B, L, E, H = (4, 64, 256, 32)
        S = E // H
        EXTRA_MAA, EXTRA_DECAY = (32, 64)
        EPS = 1e-05

        def _ln(x, w, b):
            m = jnp.mean(x, axis=-1, keepdims=True)
            v = jnp.mean((x - m) ** 2, axis=-1, keepdims=True)
            return (x - m) * jax.lax.rsqrt(v + EPS) * w + b

        def _token_shift(xn, prev_row):
            first = (prev_row - xn[:, 0])[:, None]
            rest = xn[:, :-1] - xn[:, 1:]
            return jnp.concatenate([first, rest], axis=1)
        key = jax.random.key(seed)
        ks = jax.random.split(key, 24)
        rn = lambda k, shp, s=1.0: jax.random.normal(k, shp, dtype=jnp.float32) * s
        return dict(x=rn(ks[0], (B, L, E)), state=rn(ks[1], (B, 2 + S, E), 0.1), ln1_w=jnp.ones((E,), jnp.float32), ln1_b=jnp.zeros((E,), jnp.float32), ln2_w=jnp.ones((E,), jnp.float32), ln2_b=jnp.zeros((E,), jnp.float32), maa_x=rn(ks[2], (E,), 0.02), maa_w1=rn(ks[3], (E, 5 * EXTRA_MAA), 0.02), maa_w2=rn(ks[4], (5, EXTRA_MAA, E), 0.02), maa_stack=rn(ks[5], (5, E), 0.02), time_decay=rn(ks[6], (E,), 0.5), decay_w1=rn(ks[7], (E, EXTRA_DECAY), 0.02), decay_w2=rn(ks[8], (EXTRA_DECAY, E), 0.02), faaaa=rn(ks[9], (H, S), 0.1), Wr=rn(ks[10], (E, E), 0.02), Wk=rn(ks[11], (E, E), 0.02), Wv=rn(ks[12], (E, E), 0.02), Wg=rn(ks[13], (E, E), 0.02), Wo=rn(ks[14], (E, E), 0.02), gn_w=jnp.ones((E,), jnp.float32), gn_b=jnp.zeros((E,), jnp.float32), ffn_maa_k=rn(ks[15], (E,), 0.02), ffn_maa_r=rn(ks[16], (E,), 0.02), ffn_Wk=rn(ks[17], (E, E), 0.02), ffn_Wr=rn(ks[18], (E, E), 0.02), ffn_Wv=rn(ks[19], (E, E), 0.02), i=0)
    _L1_xattn_all = _L1_xattn_setup()
    _L1_xattn_in = {k: v for k, v in _L1_xattn_all.items() if k in ('ln1_w', 'ln1_b', 'ln2_w', 'ln2_b', 'maa_x', 'maa_w1', 'maa_w2', 'maa_stack', 'time_decay', 'decay_w1', 'decay_w2', 'faaaa', 'Wr', 'Wk', 'Wv', 'Wg', 'Wo', 'gn_w', 'gn_b', 'ffn_maa_k', 'ffn_maa_r', 'ffn_Wk', 'ffn_Wr', 'ffn_Wv')}
    del _L1_xattn_all
    return {'x': x, 'ctx_2048': ctx_2048, 'L0_xattn_Wg': _L0_xattn_in['Wg'], 'L0_xattn_bg': _L0_xattn_in['bg'], 'L0_xattn_Wtheta': _L0_xattn_in['Wtheta'], 'L0_xattn_btheta': _L0_xattn_in['btheta'], 'L0_xattn_Wphi': _L0_xattn_in['Wphi'], 'L0_xattn_bphi': _L0_xattn_in['bphi'], 'L0_xattn_Wz': _L0_xattn_in['Wz'], 'L0_xattn_bz': _L0_xattn_in['bz'], 'L0_xattn_gamma': _L0_xattn_in['gamma'], 'L0_xattn_beta': _L0_xattn_in['beta'], 'L1_xattn_ln1_w': _L1_xattn_in['ln1_w'], 'L1_xattn_ln1_b': _L1_xattn_in['ln1_b'], 'L1_xattn_ln2_w': _L1_xattn_in['ln2_w'], 'L1_xattn_ln2_b': _L1_xattn_in['ln2_b'], 'L1_xattn_maa_x': _L1_xattn_in['maa_x'], 'L1_xattn_maa_w1': _L1_xattn_in['maa_w1'], 'L1_xattn_maa_w2': _L1_xattn_in['maa_w2'], 'L1_xattn_maa_stack': _L1_xattn_in['maa_stack'], 'L1_xattn_time_decay': _L1_xattn_in['time_decay'], 'L1_xattn_decay_w1': _L1_xattn_in['decay_w1'], 'L1_xattn_decay_w2': _L1_xattn_in['decay_w2'], 'L1_xattn_faaaa': _L1_xattn_in['faaaa'], 'L1_xattn_Wr': _L1_xattn_in['Wr'], 'L1_xattn_Wk': _L1_xattn_in['Wk'], 'L1_xattn_Wv': _L1_xattn_in['Wv'], 'L1_xattn_Wg': _L1_xattn_in['Wg'], 'L1_xattn_Wo': _L1_xattn_in['Wo'], 'L1_xattn_gn_w': _L1_xattn_in['gn_w'], 'L1_xattn_gn_b': _L1_xattn_in['gn_b'], 'L1_xattn_ffn_maa_k': _L1_xattn_in['ffn_maa_k'], 'L1_xattn_ffn_maa_r': _L1_xattn_in['ffn_maa_r'], 'L1_xattn_ffn_Wk': _L1_xattn_in['ffn_Wk'], 'L1_xattn_ffn_Wr': _L1_xattn_in['ffn_Wr'], 'L1_xattn_ffn_Wv': _L1_xattn_in['ffn_Wv']}

def reference(x, ctx_2048, L0_xattn_Wg, L0_xattn_bg, L0_xattn_Wtheta, L0_xattn_btheta, L0_xattn_Wphi, L0_xattn_bphi, L0_xattn_Wz, L0_xattn_bz, L0_xattn_gamma, L0_xattn_beta, L1_xattn_ln1_w, L1_xattn_ln1_b, L1_xattn_ln2_w, L1_xattn_ln2_b, L1_xattn_maa_x, L1_xattn_maa_w1, L1_xattn_maa_w2, L1_xattn_maa_stack, L1_xattn_time_decay, L1_xattn_decay_w1, L1_xattn_decay_w2, L1_xattn_faaaa, L1_xattn_Wr, L1_xattn_Wk, L1_xattn_Wv, L1_xattn_Wg, L1_xattn_Wo, L1_xattn_gn_w, L1_xattn_gn_b, L1_xattn_ffn_maa_k, L1_xattn_ffn_maa_r, L1_xattn_ffn_Wk, L1_xattn_ffn_Wr, L1_xattn_ffn_Wv):
    import jax
    import jax.numpy as jnp

    def _L0_xattn_ref(x_this, x_other, Wg, bg, Wtheta, btheta, Wphi, bphi, Wz, bz, gamma, beta):
        import jax, jax.numpy as jnp
        import numpy as np
        B, C, CI, T = (8, 64, 32, 256)
        EPS = 1e-05
        g_x = jnp.einsum('oc,bct->bto', Wg, x_this) + bg
        theta = jnp.einsum('oc,bct->bot', Wtheta, x_this) + btheta[None, :, None]
        phi = jnp.einsum('oc,bct->bot', Wphi, x_other) + bphi[None, :, None]
        f = jnp.einsum('bci,bcj->bij', phi, theta)
        f_div_C = jax.nn.softmax(f, axis=-1)
        y = jnp.einsum('bij,bjo->bio', f_div_C, g_x)
        w_y = jnp.einsum('oc,btc->bot', Wz, y) + bz[None, :, None]
        mean = jnp.mean(w_y, axis=(0, 2), keepdims=True)
        var = jnp.var(w_y, axis=(0, 2), keepdims=True)
        w_y = gamma[None, :, None] * (w_y - mean) * jax.lax.rsqrt(var + EPS) + beta[None, :, None]
        return w_y + x_this

    def _L1_xattn_ref(x, state, ln1_w, ln1_b, ln2_w, ln2_b, maa_x, maa_w1, maa_w2, maa_stack, time_decay, decay_w1, decay_w2, faaaa, Wr, Wk, Wv, Wg, Wo, gn_w, gn_b, ffn_maa_k, ffn_maa_r, ffn_Wk, ffn_Wr, ffn_Wv, i):
        import jax, jax.numpy as jnp
        import numpy as np
        B, L, E, H = (4, 64, 256, 32)
        S = E // H
        EXTRA_MAA, EXTRA_DECAY = (32, 64)
        EPS = 1e-05

        def _ln(x, w, b):
            m = jnp.mean(x, axis=-1, keepdims=True)
            v = jnp.mean((x - m) ** 2, axis=-1, keepdims=True)
            return (x - m) * jax.lax.rsqrt(v + EPS) * w + b

        def _token_shift(xn, prev_row):
            first = (prev_row - xn[:, 0])[:, None]
            rest = xn[:, :-1] - xn[:, 1:]
            return jnp.concatenate([first, rest], axis=1)
        b, l = (x.shape[0], x.shape[1])
        i0 = (2 + S) * i + 0
        i1 = (2 + S) * i + 1
        xn = _ln(x, ln1_w, ln1_b)
        sx = _token_shift(xn, state[:, i1])
        xxx = jnp.tanh((xn + sx * maa_x) @ maa_w1).reshape(b, l, 5, 1, EXTRA_MAA)
        xxx = jnp.matmul(xxx, maa_w2).reshape(b, l, 5, E)
        x5 = xn[:, :, None] + sx[:, :, None] * (maa_stack + xxx)
        w = jnp.exp(-jnp.exp(time_decay + jnp.tanh(x5[:, :, 1] @ decay_w1) @ decay_w2))
        w = w.reshape(b, l, H, S)
        r = (x5[:, :, 3] @ Wr.T).reshape(b, l, H, S)
        k = (x5[:, :, 0] @ Wk.T).reshape(b, l, H, S)
        v = (x5[:, :, 2] @ Wv.T).reshape(b, l, H, S)
        g = jax.nn.silu(x5[:, :, 4] @ Wg.T)
        s0 = state[:, (2 + S) * i + 2:(2 + S) * (i + 1)].reshape(b, H, S, S)
        u = faaaa[None, :, :, None]

        def step(s, rkvw):
            r_t, k_t, v_t, w_t = rkvw
            a = k_t[:, :, :, None] * v_t[:, :, None, :]
            out = jnp.einsum('bhk,bhkd->bhd', r_t, u * a + s)
            return (a + w_t[:, :, :, None] * s, out)
        xs = tuple((jnp.moveaxis(t, 1, 0) for t in (r, k, v, w)))
        _, outs = jax.lax.scan(step, s0, xs)
        att = jnp.moveaxis(outs, 0, 1).reshape(b, l, E)
        a4 = att.reshape(b, l, H, S)
        m = jnp.mean(a4, axis=-1, keepdims=True)
        var = jnp.mean((a4 - m) ** 2, axis=-1, keepdims=True)
        att = ((a4 - m) * jax.lax.rsqrt(var + EPS)).reshape(b, l, E) * gn_w + gn_b
        x = x + att * g @ Wo.T
        xn2 = _ln(x, ln2_w, ln2_b)
        sx2 = _token_shift(xn2, state[:, i0])
        xk = xn2 + sx2 * ffn_maa_k
        xr = xn2 + sx2 * ffn_maa_r
        rr = jax.nn.sigmoid(xr @ ffn_Wr.T)
        kk = jnp.square(jax.nn.relu(xk @ ffn_Wk.T))
        x = x + rr * (kk @ ffn_Wv.T)
        return x
    x = _L0_xattn_ref(x, ctx_2048, L0_xattn_Wg, L0_xattn_bg, L0_xattn_Wtheta, L0_xattn_btheta, L0_xattn_Wphi, L0_xattn_bphi, L0_xattn_Wz, L0_xattn_bz, L0_xattn_gamma, L0_xattn_beta)
    x = _L1_xattn_ref(x, ctx_2048, L1_xattn_ln1_w, L1_xattn_ln1_b, L1_xattn_ln2_w, L1_xattn_ln2_b, L1_xattn_maa_x, L1_xattn_maa_w1, L1_xattn_maa_w2, L1_xattn_maa_stack, L1_xattn_time_decay, L1_xattn_decay_w1, L1_xattn_decay_w2, L1_xattn_faaaa, L1_xattn_Wr, L1_xattn_Wk, L1_xattn_Wv, L1_xattn_Wg, L1_xattn_Wo, L1_xattn_gn_w, L1_xattn_gn_b, L1_xattn_ffn_maa_k, L1_xattn_ffn_maa_r, L1_xattn_ffn_Wk, L1_xattn_ffn_Wr, L1_xattn_ffn_Wv, 0)
    return x

_drawn_inputs = setup_inputs


def setup_inputs(seed=0):
    import zlib

    import numpy as np

    out = dict(_drawn_inputs(seed))
    spreads = {'L0_xattn_bg': (0.0, 0.8),
     'L0_xattn_btheta': (0.0, 0.8),
     'L0_xattn_bphi': (0.0, 0.1),
     'L0_xattn_bz': (0.0, 0.8),
     'L1_xattn_ln1_w': (1.0, 0.6),
     'L1_xattn_ln1_b': (0.0, 0.8),
     'L1_xattn_ln2_w': (1.0, 0.6),
     'L1_xattn_ln2_b': (0.0, 0.8),
     'L1_xattn_gn_w': (1.0, 0.6),
     'L1_xattn_gn_b': (0.0, 0.8)}
    factors = {'L1_xattn_maa_x': 8.0,
     'L1_xattn_maa_w1': 8.0,
     'L1_xattn_maa_w2': 8.0,
     'L1_xattn_maa_stack': 8.0,
     'L1_xattn_time_decay': 4.757,
     'L1_xattn_decay_w1': 8.0,
     'L1_xattn_decay_w2': 8.0,
     'L1_xattn_faaaa': 8.0,
     'L1_xattn_ffn_maa_k': 8.0,
     'L1_xattn_ffn_maa_r': 8.0,
     'L1_xattn_ffn_Wk': 4.928,
     'L1_xattn_ffn_Wr': 8.0,
     'L1_xattn_ffn_Wv': 4.555}
    for name, (base, spread) in spreads.items():
        noise = np.random.default_rng([zlib.crc32(name.encode()), seed]).standard_normal(out[name].shape)
        drawn = base * np.exp(spread * noise) if base else spread * noise
        out[name] = jnp.asarray(drawn.astype(out[name].dtype))
    for name, factor in factors.items():
        out[name] = (out[name] * factor).astype(out[name].dtype)
    return out
```

```python
from contextlib import ExitStack

import concourse.bass as bass
from concourse import mybir

F32 = mybir.dt.float32
ALU = mybir.AluOpType
ACT = mybir.ActivationFunctionType
AX = mybir.AxisListType
P = 128

B, C, T, CI = 64, 64, 256, 32
L, E, H, S = C, T, 32, 8
EPS = 1e-5
PAIRS = B // 2
QUADS = B // 4
NB = 8
CHUNKS = B // NB
TOK = NB * L
TILES = TOK // P
EC = E // P
L1 = L + 1
MIX, DEC = 32, 64

(LN1W, LN1B, LN2W, LN2B, MAAX, STK0, TDEC, BONUS, GNW, GNB, FMK, FMR) = (0, 1, 2, 3, 4, 5, 10, 11, 12, 13, 14, 15)
WR, WK, WV, WG, WO, FK, FR, FV = range(8)
C_PROD, C_SELF, C_ONES, C_AVG, C_HALF, C_ID = 0, 8, 9, 10, 11, 12


def wait(eng, sem, value):
    if isinstance(value, int) and value <= 0:
        return
    eng.wait_ge(sem, value)


def wait_apart(nc, dve, sem, value, spare):
    dve.wait_ge(sem, value)
    if not isinstance(value, int):
        nc.vector.memset(spare, 0.0)


def attention(nc, sem, t, d):
    s_xin = [sem("pair_even_in"), sem("pair_odd_in")]
    s_w = sem("weights_in")
    s_zero = sem("blockdiag_zeroed")
    s_bd = sem("blockdiag_in")
    s_wc, s_wcs = sem("gz_weight_done"), sem("gz_weight_ready")
    s_bgb = sem("bg_spread")
    s_proj, s_gz = sem("thetaphi_done"), sem("gz_done")
    s_thph, s_gzr = sem("thetaphi_ready"), sem("gz_ready")
    s_f, s_max, s_exp = sem("scores_done"), sem("negmax_ready"), sem("exp_ready")
    s_rec, s_scl = sem("rowsum_inverted"), sem("probs_scaled")
    s_t, s_pta, s_ptd = sem("probsT_done"), sem("probsT_even_ready"), sem("probsT_odd_ready")
    s_av, s_wy, s_bn = sem("av_done"), sem("wy_ready"), sem("stats_ready")
    wyz, stats, cst = t["wyz"], t["stats"], t["cst"]
    ident = cst[:, C_ID, :]

    ctx = ExitStack()
    with ctx:
        def sb(name, shape):
            return ctx.enter_context(nc.sbuf_tensor(name, shape, F32))

        def pb(name):
            return ctx.enter_context(nc.psum_tensor(name, [P, 512], F32))

        x2 = [sb(f"x2_{p}", [P, T]) for p in range(2)]
        c2 = [sb(f"c2_{p}", [P, T]) for p in range(2)]
        bd_th, bd_ph, bd_gz = sb("bd_th", [P, 2 * CI]), sb("bd_ph", [P, 2 * CI]), sb("bd_gz", [P, 2 * C])
        bth, bph = sb("bth", [2 * CI, 1]), sb("bph", [2 * CI, 1])
        wg, wzT, bg, bz = sb("wg", [CI, C]), sb("wzT", [CI, C]), sb("bg", [CI, 1]), sb("bz", [1, C])
        bgb, ones = sb("bgb", [CI, P]), sb("ones", [CI, P])
        gzb = sb("gzb", [P, C])
        thph = [sb(f"thph{p}", [2 * CI, 2 * T]) for p in range(2)]
        gz = [sb(f"gz{p}", [P, 2, 2, C]) for p in range(2)]
        pr = [sb(f"probs{b}", [P, 2, T]) for b in range(4)]
        pT = [sb(f"probsT{b}", [P, 2, T]) for b in range(4)]
        nm = [sb(f"negmax{b}", [P, 2]) for b in range(4)]
        rs = [sb(f"rowsum{b}", [P, 2]) for b in range(4)]
        ri = [sb(f"rowinv{b}", [P, 3]) for b in range(4)]
        ps_proj, ps_gz = pb("ps_proj"), pb("ps_gz")
        ps_f, ps_t, ps_av = [pb("ps_f0"), pb("ps_f1")], [pb("ps_t0"), pb("ps_t1")], [pb("ps_av0"), pb("ps_av1")]
        block = ctx.enter_context(nc.Block())

        @block.sync
        def _(sp):
            def load_pair(pi, p):
                sp.dma_start(x2[p][:, :], d["x"][pi, :, :]).then_inc(s_xin[p], 16)
                sp.dma_start(c2[p][:, :], d["ctx"][pi, :, :]).then_inc(s_xin[p], 16)

            sp.dma_start(cst[:, :, :], d["cst"]).then_inc(s_w, 16)
            for dst, src in ((wg, d["Wg"]), (wzT, d["WzT"]), (bg, d["bg"]), (bz, d["bz"]), (bth, d["bth"]), (bph, d["bph"])):
                sp.dma_start(dst[:, :], src).then_inc(s_w, 16)
            sp.wait_ge(s_zero, 3)
            for b in range(2):
                sp.dma_start(bd_th[C * b:C * b + C, CI * b:CI * b + CI], d["WthT"]).then_inc(s_bd, 16)
                sp.dma_start(bd_ph[C * b:C * b + C, CI * b:CI * b + CI], d["WphT"]).then_inc(s_bd, 16)
            load_pair(0, 0)
            load_pair(1, 1)
            for dst, src in ((t["vec"], d["vec"]), (t["bnv"], d["bnv"]), (t["wsq"], d["wsq"]), (t["w1"], d["w1"]),
                             (t["w2"], d["w2"][0:P, :]), (t["dw1"], d["dw1"]), (t["s0"], d["s0"]),
                             (t["prev1"], d["prev1"]), (t["prev0"], d["prev0"])):
                sp.dma_start(dst[(slice(None),) * len(dst.shape)], src).then_inc(t["s_late"], 16)
            sp.dma_start(t["low_w"][0:MIX, :], d["w2"][P:P + MIX, :]).then_inc(t["s_late"], 16)
            sp.dma_start(t["low_w"][DEC:2 * DEC, :], d["dw2"]).then_inc(t["s_late"], 16)
            with sp.Fori(1, QUADS) as q:
                for p in range(2):
                    sp.wait_ge(s_gz, q * 2 + p - 1)
                    sp.dma_start(x2[p][:, :], d["x"][bass.ds(q * 2 + p, 1)].rearrange("a p f -> p (a f)")).then_inc(s_xin[p], 16)
                    sp.dma_start(c2[p][:, :], d["ctx"][bass.ds(q * 2 + p, 1)].rearrange("a p f -> p (a f)")).then_inc(s_xin[p], 16)

        @block.gpsimd
        def _(pool):
            for m in (bd_th, bd_ph, bd_gz):
                nc.gpsimd.memset(m[:, :], 0.0).then_inc(s_zero, 1)
            nc.gpsimd.memset(ones[:, :], 1.0).then_inc(s_zero, 1)

        @block.tensor
        def _(pe):
            def proj(pi, p, q):
                pe.wait_ge(s_xin[p], q * 32 + 32)
                wait(pe, s_thph, pi * 2)
                nc.tensor.matmul(ps_proj[0:2 * CI, 0:T], bd_th[:, :], x2[p][:, :], start=True, stop=True)
                nc.tensor.matmul(ps_proj[0:2 * CI, T:2 * T], bd_ph[:, :], c2[p][:, :], start=True, stop=True).then_inc(s_proj, 1)
                wait(pe, s_gzr, pi)
                for j in range(2):
                    mm = nc.tensor.matmul(ps_gz[:, P * j:P * j + P], x2[p][:, P * j:P * j + P], bd_gz[:, :], start=True, stop=True)
                mm.then_inc(s_gz, 1)

            def scores(g, b, pi):
                pe.wait_ge(s_thph, pi * 2 + 2)
                wait(pe, s_exp, g - 1)
                r = CI * (b % 2)
                tp = thph[(b // 2) % 2]
                for i in range(2):
                    mm = nc.tensor.matmul(ps_f[b % 2][:, T * i:T * i + T], tp[r:r + CI, T + P * i:T + P * i + P],
                                          tp[r:r + CI, 0:T], start=True, stop=True)
                mm.then_inc(s_f, 1)

            def transposes(g, b, half):
                pe.wait_ge(s_scl, g * 2 + 2)
                wait(pe, (s_pta, s_ptd)[b % 2], half)
                for j in range(2):
                    for i in range(2):
                        mm = nc.tensor.transpose(ps_t[b % 2][:, T * j + P * i:T * j + P * i + P],
                                                 pr[b][:, i, P * j:P * j + P], ident)
                mm.then_inc(s_t, 1)

            def attend(g, b, pi):
                pe.wait_ge((s_pta, s_ptd)[b % 2], pi + 1)
                pe.wait_ge(s_gzr, pi + 1)
                if b % 2 == 0:
                    wait(pe, s_wy, pi - 1)
                r = C * (b % 2)
                for j in range(2):
                    mm = nc.tensor.matmul(ps_av[b // 2][r:r + C, 0:T], gz[b // 2][:, j, b % 2, :], pT[b][:, j, :],
                                          start=(j == 0), stop=(j == 1))
                mm.then_inc(s_av, 1)

            def slot(q, b, first=False, last=False):
                g = q * 4 + b
                if not (last and b >= 2):
                    scores(g + 2, (b + 2) % 4, q * 2 + (b + 2) // 2)
                if b % 2 and not last:
                    proj(q * 2 + (b + 3) // 2, ((b + 3) // 2) % 2, q + 1)
                transposes(g, b, q * 2 + b // 2)
                if not (first and b == 0):
                    attend(g - 1, (b - 1) % 4, q * 2 + (b - 1) // 2)

            pe.wait_ge(s_w, 16 * 7)
            pe.wait_ge(s_bgb, 1)
            pe.wait_ge(s_zero, 4)
            nc.tensor.matmul(ps_gz[0:C, 0:C], wg[:, :], wzT[:, :], start=True, stop=True)
            nc.tensor.matmul(ps_gz[C:2 * C, 0:C], wg[:, :], wzT[:, :], start=True, stop=True)
            nc.tensor.matmul(ps_proj[:, 0:C], bgb[:, :], wzT[:, :], start=True, stop=False)
            nc.tensor.matmul(ps_proj[:, 0:C], ones[0:1, :], bz[:, :], start=False, stop=True).then_inc(s_wc, 1)
            pe.wait_ge(s_wcs, 3)
            pe.wait_ge(s_bd, 64)
            proj(0, 0, 0)
            scores(0, 0, 0)
            scores(1, 1, 0)
            proj(1, 1, 0)
            for b in range(4):
                slot(0, b, first=True)
            with pe.Fori(1, QUADS - 1) as q:
                for b in range(4):
                    slot(q, b)
            for b in range(4):
                slot(QUADS - 1, b, last=True)
            attend(B - 1, 3, PAIRS - 1)

        @block.scalar
        def _(act):
            def exps(g, b):
                act.wait_ge(s_max, g + 1)
                wait(act, s_t, g - 3)
                for i in range(2):
                    e = nc.scalar.activation(pr[b][:, i, :], ps_f[b % 2][:, T * i:T * i + T], ACT.Exp,
                                             bias=nm[b][:, i:i + 1], accum_out=rs[b][:, i:i + 1])
                e.then_inc(s_exp, 1)

            def theta_phi(pi, p, g):
                act.wait_ge(s_proj, pi + 1)
                wait(act, s_f, g + 1)
                nc.scalar.activation(thph[p][:, 0:T], ps_proj[0:2 * CI, 0:T], ACT.Identity, bias=bth[:, 0:1]).then_inc(s_thph, 1)
                nc.scalar.activation(thph[p][:, T:2 * T], ps_proj[0:2 * CI, T:2 * T], ACT.Identity, bias=bph[:, 0:1]).then_inc(s_thph, 1)

            def probs_t(g, b):
                act.wait_ge(s_t, g + 1)
                wait(act, s_av, g - 3)
                nc.scalar.activation(pT[b][:, :, :], ps_t[b % 2][:, :].rearrange("p (j i) -> p j i", j=2), ACT.Copy).then_inc(s_pta, 1)

            def w_y(pi, p):
                act.wait_ge(s_av, pi * 2 + 2)
                nc.scalar.activation(wyz[:, bass.ds(pi, 1), :], ps_av[p][:, 0:T].rearrange("p (a f) -> p a f", a=1), ACT.Copy).then_inc(s_wy, 1)

            def slot(q, b, first=False, last=False):
                g = q * 4 + b
                if not (last and b >= 2):
                    exps(g + 2, (b + 2) % 4)
                if b % 2:
                    if not last:
                        theta_phi(q * 2 + (b + 3) // 2, ((b + 3) // 2) % 2, g)
                else:
                    probs_t(g, b)
                    if not (first and b == 0):
                        w_y(q * 2 + (b - 2) // 2, (b // 2 + 1) % 2)

            act.wait_ge(s_wc, 1)
            nc.scalar.copy(bd_gz[0:C, 0:C], ps_gz[0:C, 0:C]).then_inc(s_wcs, 1)
            nc.scalar.copy(bd_gz[C:2 * C, C:2 * C], ps_gz[C:2 * C, 0:C]).then_inc(s_wcs, 1)
            nc.scalar.copy(gzb[:, :], ps_proj[:, 0:C]).then_inc(s_wcs, 1)
            theta_phi(0, 0, -1)
            exps(0, 0)
            exps(1, 1)
            theta_phi(1, 1, -1)
            for b in range(4):
                slot(0, b, first=True)
            with act.Fori(1, QUADS - 1) as q:
                for b in range(4):
                    slot(q, b)
            for b in range(4):
                slot(QUADS - 1, b, last=True)
            w_y(PAIRS - 1, 1)

        @block.vector
        def _(dve):
            def negmax(g, b):
                dve.wait_ge(s_f, g + 1)
                nc.vector.tensor_reduce(nm[b][:, :], ps_f[b % 2][:, :].rearrange("p (i j) -> p i j", i=2), AX.X, ALU.max,
                                        negate=True).then_inc(s_max, 1)

            def scale(g, b):
                dve.wait_ge(s_exp, g + 1)
                nc.vector.reciprocal(ri[b][:, 0:2], rs[b][:, :]).then_inc(s_rec, 1)
                dve.wait_ge(s_rec, g + 1)
                for i in range(2):
                    nc.vector.tensor_scalar(pr[b][:, i, :], pr[b][:, i, :], ri[b][:, i:i + 1], None, ALU.mult).then_inc(s_scl, 1)

            def probs_t(g, b):
                dve.wait_ge(s_t, g + 1)
                wait(dve, s_av, g - 3)
                nc.vector.tensor_copy(pT[b][:, :, :], ps_t[b % 2][:, :].rearrange("p (j i) -> p j i", j=2)).then_inc(s_ptd, 1)

            def gz_out(pi, p, g):
                dve.wait_ge(s_gz, pi + 1)
                wait(dve, s_av, g - 1)
                nc.vector.tensor_tensor(gz[p][:, :, :, :].rearrange("p j b c -> p (j b) c"),
                                        ps_gz[:, 0:T].rearrange("p (j c) -> p j c", c=C),
                                        gzb[:, :].rearrange("p (a c) -> p a c", a=1).broadcast_to([P, 4, C]), ALU.add).then_inc(s_gzr, 1)

            def statistics(pi):
                wait_apart(nc, dve, s_wy, pi + 1, ri[0][:, 2:3])
                nc.vector.bn_stats(stats[:, bass.ds(pi, 1), :].rearrange("p a s -> p (a s)"),
                                   wyz[:, bass.ds(pi, 1), :].rearrange("p a f -> p (a f)")).then_inc(s_bn, 1)

            def slot(q, b, first=False, last=False):
                g = q * 4 + b
                if b % 2 and not (last and b == 3):
                    gz_out(q * 2 + (b + 1) // 2, ((b + 1) // 2) % 2, g)
                if not (last and b >= 2):
                    negmax(g + 2, (b + 2) % 4)
                if not (last and b == 3):
                    scale(g + 1, (b + 1) % 4)
                if b % 2:
                    probs_t(g, b)
                    if not (first and b == 1):
                        statistics(q * 2 + (b - 3) // 2)

            dve.wait_ge(s_w, 16 * 7)
            dve.wait_ge(s_zero, 4)
            nc.vector.tensor_scalar(bgb[:, :], ones[:, :], bg[:, 0:1], None, ALU.mult).then_inc(s_bgb, 1)
            negmax(0, 0)
            negmax(1, 1)
            dve.wait_ge(s_wcs, 3)
            gz_out(0, 0, 0)
            scale(0, 0)
            for b in range(4):
                slot(0, b, first=True)
            with dve.Fori(1, QUADS - 1) as q:
                for b in range(4):
                    slot(q, b)
            for b in range(4):
                slot(QUADS - 1, b, last=True)
            statistics(PAIRS - 1)
            dve.wait_ge(s_bn, PAIRS)


def norm_params(nc, sem, t):
    s_loc, s_mean, s_dev, s_var = sem("local_moments"), sem("mean_done"), sem("deviation_ready"), sem("var_done")
    s_ve, s_pw, s_par, s_half = sem("var_eps_ready"), sem("bn_rstd_ready"), sem("bn_params_ready"), sem("pow_exponent_ready")
    ctx = ExitStack()
    with ctx:
        mv = ctx.enter_context(nc.sbuf_tensor("mv", [P, 8], F32))
        ps = ctx.enter_context(nc.psum_tensor("ps_bn", [P, 512], F32))
        ps2 = ctx.enter_context(nc.psum_tensor("ps_bn2", [P, 512], F32))
        block = ctx.enter_context(nc.Block())
        half = t["cst"][:, C_HALF, :]

        @block.tensor
        def _(pe):
            pe.wait_ge(s_loc, 1)
            nc.tensor.matmul(ps[:, 0:2], half, mv[:, 0:2], start=True, stop=True).then_inc(s_mean, 1)
            pe.wait_ge(s_dev, 4)
            nc.tensor.matmul(ps2[:, 0:2], half, mv[:, 4:6], start=True, stop=True).then_inc(s_var, 1)

        @block.gpsimd
        def _(pool):
            nc.gpsimd.memset(t["mhalf"][:, :], -0.5).then_inc(s_half, 1)
            pool.wait_ge(s_half, 1)
            pool.wait_ge(s_ve, 1)
            nc.gpsimd.tensor_tensor(mv[:, 6:7], mv[:, 6:7], t["mhalf"][:, 0:1], ALU.pow).then_inc(s_pw, 1)

        @block.vector
        def _(dve):
            nc.vector.bn_aggr(mv[:, 0:2], t["stats"][:, :, :].rearrange("p a s -> p (a s)")).then_inc(s_loc, 1)
            dve.wait_ge(s_mean, 1)
            nc.vector.tensor_copy(mv[:, 2:3], ps[:, 0:1]).then_inc(s_dev, 1)
            dve.wait_ge(s_dev, 1)
            nc.vector.tensor_tensor(mv[:, 3:4], mv[:, 0:1], mv[:, 2:3], ALU.subtract).then_inc(s_dev, 1)
            dve.wait_ge(s_dev, 2)
            nc.vector.tensor_tensor(mv[:, 5:6], mv[:, 3:4], mv[:, 3:4], ALU.mult).then_inc(s_dev, 1)
            dve.wait_ge(s_dev, 3)
            nc.vector.tensor_tensor(mv[:, 4:5], mv[:, 1:2], mv[:, 5:6], ALU.add).then_inc(s_dev, 1)
            dve.wait_ge(s_var, 1)
            nc.vector.tensor_scalar(mv[:, 6:7], ps2[:, 0:1], EPS, None, ALU.add).then_inc(s_ve, 1)
            dve.wait_ge(s_pw, 1)
            dve.wait_ge(t["s_late"], 16 * 11)
            nc.vector.tensor_tensor(t["bna"][:, :], mv[:, 6:7], t["bnv"][:, 0:1], ALU.mult).then_inc(s_par, 1)
            dve.wait_ge(s_par, 1)
            nc.vector.tensor_tensor(mv[:, 7:8], mv[:, 2:3], t["bna"][:, :], ALU.mult).then_inc(s_par, 1)
            dve.wait_ge(s_par, 2)
            nc.vector.tensor_tensor(t["bnb"][:, :], t["bnv"][:, 1:2], mv[:, 7:8], ALU.subtract).then_inc(s_par, 1)
            dve.wait_ge(s_par, 3)


def rwkv(nc, sem, t, d, out):
    wyz, cst, vec, wsq, low_w = t["wyz"], t["cst"], t["vec"], t["wsq"], t["low_w"]
    ident, ones_head, avg_head = cst[:, C_ID, :], cst[:, C_ONES, :], cst[:, C_AVG, :]

    def col(v, c):
        return vec[:, v, c:c + 1]

    x_in, x_biased, z_ready = sem("x_in"), sem("x_biased"), sem("z_ready")
    st1, mv1_s, ln1_var, ln1_rstd, zn_ready = sem("ln1_stats"), sem("ln1_moments"), sem("ln1_var"), sem("ln1_rstd"), sem("zn_ready")
    xn_ready, xprev, sx_ready, xm_ready = sem("xn_ready"), sem("xprev_ready"), sem("sx_ready"), sem("xm_ready")
    mix_tanh, mod_ready, x5_ready = sem("mix_tanh"), sem("modulated"), sem("x5_ready")
    dec_tanh, dec_exp, w_ready = sem("decay_tanh"), sem("decay_exp"), sem("w_ready")
    v_ready, k_ready, r_ready, g_tanh, gate_ready = sem("v_ready"), sem("k_ready"), sem("r_ready"), sem("gate_tanh"), sem("gate_ready")
    a_done = sem("a_matmuls_done")
    v_spread = [sem("v_spread_0"), sem("v_spread_1")]
    ruk_ready, head_sum, bonus_ready = sem("ruk_ready"), sem("head_sum_done"), sem("bonus_ready")
    kv_ready, scanned, prod_ready, prod_used, att_done = sem("kv_ready"), sem("scanned"), sem("prod_ready"), sem("prod_used"), sem("att_done")
    att_sq, var_ln, gn_rstd, gn_scaled, ag_ready = sem("att_squared"), sem("var_ln"), sem("gn_rstd"), sem("att_scaled"), sem("att_gated")
    x1_ready, st2, mv2_s, ln2_var, ln2_rstd, zn2_ready = sem("x1_ready"), sem("ln2_stats"), sem("ln2_moments"), sem("ln2_var"), sem("ln2_rstd"), sem("zn2_ready")
    xn2_ready, xprev2, sx2_ready, xk_ready, xr_ready = sem("xn2_ready"), sem("xprev2_ready"), sem("sx2_ready"), sem("xk_ready"), sem("xr_ready")
    relu_ready, kk_ready, rr_ready, y_mid, out_ready, stored = sem("relu_ready"), sem("kk_ready"), sem("rr_ready"), sem("y_mid"), sem("out_ready"), sem("out_stored")
    c_done = sem("c_matmuls_done")
    init_done = sem("init_done")

    A_ORDER = ["T0", "T1", "m0", "m1", "w0a", "w0b", "w1a", "w1b", "dec1", "w2a", "w2b", "dec2a", "dec2b", "v0", "v1",
               "w3a", "w3b", "k0", "k1", "w4a", "w4b", "r0", "r1", "g0", "g1"]
    A_READ = {"T0": (xn_ready, 1, 2), "T1": (xn_ready, 2, 2), "m0": (mix_tanh, 1, 2), "m1": (mix_tanh, 2, 2),
              "dec1": (dec_tanh, 1, 1), "dec2a": (dec_exp, 1, 2), "dec2b": (dec_exp, 2, 2),
              "v0": (v_ready, 1, 2), "v1": (v_ready, 2, 2), "k0": (k_ready, 1, 2), "k1": (k_ready, 2, 2),
              "r0": (r_ready, 1, 2), "r1": (r_ready, 2, 2), "g0": (gate_ready, 1, 2), "g1": (gate_ready, 2, 2)}
    for j in range(5):
        A_READ[f"w{j}a"], A_READ[f"w{j}b"] = (mod_ready, 2 * j + 1, 10), (mod_ready, 2 * j + 2, 10)
    NA = len(A_ORDER)
    C_ORDER = ["var0", "var1", "o0", "o1", "T0", "T1", "k0", "k1", "r0", "r1", "v0", "v1"]
    C_READ = {"var0": (var_ln, 1, 2), "var1": (var_ln, 2, 2), "o0": (x1_ready, 1, 2), "o1": (x1_ready, 2, 2),
              "T0": (xn2_ready, 1, 2), "T1": (xn2_ready, 2, 2), "k0": (relu_ready, 1, 2), "k1": (relu_ready, 2, 2),
              "r0": (rr_ready, 1, 2), "r1": (rr_ready, 2, 2), "v0": (y_mid, 1, 2), "v1": (y_mid, 2, 2)}
    NC = len(C_ORDER)
    MIX_OF = [1, 2, 0, 3, 4]
    X5_READ_BY = ["dec1", "v1", "k1", "r1", "g1"]

    ctx = ExitStack()
    with ctx:
        def sb(name, shape):
            return ctx.enter_context(nc.sbuf_tensor(name, shape, F32))

        def pb(name):
            return ctx.enter_context(nc.psum_tensor(name, [P, 512], F32))

        eps = sb("eps", [P, 2])
        xr_in = sb("x_chunk", [P, TILES, E])
        zn = sb("zn", [P, TILES * E])
        xm = zn
        zn2 = sb("zn2", [P, TILES * E])
        st1b, mv1, ve1, rs1 = sb("st1", [P, TILES, 6]), sb("mv1", [P, TILES, 2]), sb("ve1", [P, TILES]), sb("rs1", [P, TILES])
        st2b, mv2, ve2, rs2 = sb("st2", [P, TILES, 6]), sb("mv2", [P, TILES, 2]), sb("ve2", [P, TILES]), sb("rs2", [P, TILES])
        xn, xn2 = sb("xn", [P, EC * NB, L1]), sb("xn2", [P, EC * NB, L1])
        sx = sb("sx", [P, EC * NB, L])
        sx2 = sb("sx2", [P, EC * NB, L])
        y = sx2[:, :, :].rearrange("p a b -> p (a b)").rearrange("p (m f) -> p m f", m=TILES)
        t1 = sb("mix_t", [P, TOK])
        low_t = sb("low_t", [P, TOK])
        x5 = [sb(f"x5_{i}", [P, EC * NB, L]) for i in range(2)]
        w = [[sb(f"w_{p}{h}", [P, NB, L1]) for h in range(2)] for p in range(2)]
        r = [[sb(f"r_{p}{h}", [P, TOK]) for h in range(2)] for p in range(2)]
        k = [[sb(f"k_{p}{h}", [P, TOK]) for h in range(2)] for p in range(2)]
        v = [sb(f"v_{h}", [P, TOK]) for h in range(2)]
        gate = [[sb(f"gate_{p}{h}", [P, TOK]) for h in range(2)] for p in range(2)]
        vb = [sb(f"vb_{h}", [P, S, TOK]) for h in range(2)]
        st = sb("state", [P, 4, NB, L1])
        bon = [sb(f"bonus_{h}", [P, TOK]) for h in range(2)]
        sq = [sb(f"sq_{h}", [P, TOK]) for h in range(2)]
        ag = sb("ag", [P, 2, TOK])
        rr = ag[:, :, :].rearrange("p h t -> p (h t)").rearrange("p (m f) -> p m f", m=TILES)
        xrr = sb("xr", [P, EC, TOK])
        kk = sb("kk", [P, EC, TOK])
        abank = [pb(f"ps_a{i}") for i in range(3)]
        cbank = [pb(f"ps_c{i}") for i in range(2)]
        sbank = pb("ps_headsum")
        att = [pb(f"ps_att{h}") for h in range(2)]
        block = ctx.enter_context(nc.Block())

        def bt(ap):
            return ap.rearrange("p (b t) -> p b t", t=L)

        def ab(name):
            return abank[A_ORDER.index(name) % 3]

        def cb(name):
            return cbank[C_ORDER.index(name) % 2]

        def a_at(n, name):
            return n * NA + A_ORDER.index(name) + 1

        def c_at(n, name):
            return n * NC + C_ORDER.index(name) + 1

        @block.sync
        def _(sp):
            def load_x(n):
                wait(sp, z_ready, n)
                sp.dma_start(xr_in[:, :, :], d["x"][bass.ds(n * TILES, TILES)].rearrange("a p f -> p a f")).then_inc(x_in, 16)

            def spread_v(n, h):
                sp.wait_ge(v_ready, n * 2 + h + 1)
                wait(sp, prod_used, n * 4 + 2 * h - 2)
                for i in range(S):
                    sp.dma_start(vb[h][i:P:S, :, :], v[h][:, :]).then_inc(v_spread[h], 16)

            def store(n):
                sp.wait_ge(out_ready, n * 2 + 2)
                sp.dma_start(out[bass.ds(n * TILES, TILES)].rearrange("a p f -> p a f"), y).then_inc(stored, 16)

            def body(n, c=True, a=True, x=True):
                if x:
                    load_x(n + 2)
                if a:
                    spread_v(n + 1, 0)
                if c:
                    store(n - 1)
                if a:
                    spread_v(n + 1, 1)

            load_x(0)
            load_x(1)
            spread_v(0, 0)
            spread_v(0, 1)
            body(0, c=False)
            with sp.Fori(1, CHUNKS - 2) as n:
                body(n)
            body(CHUNKS - 2, x=False)
            body(CHUNKS - 1, a=False, x=False)
            store(CHUNKS - 1)
            sp.wait_ge(stored, 16 * CHUNKS + 16)

        @block.gpsimd
        def _(pool):
            def rstd(n, var_sem, sem_out, src, dst):
                pool.wait_ge(var_sem, n + 1)
                nc.gpsimd.tensor_tensor(dst[:, :], src[:, :], t["mhalf"][:, :], ALU.pow).then_inc(sem_out, 1)

            def prev(n, shift_sem, sem_out, src, dst):
                wait(pool, shift_sem, n)
                for c in range(EC):
                    nc.gpsimd.tensor_copy(dst[:, NB * c:NB * c + NB, 0], src[:, c, bass.ds(n * NB, NB)]).then_inc(sem_out, 1)

            def add_x(n, j):
                pool.wait_ge(mod_ready, n * 10 + 2 * j + 2)
                nc.gpsimd.tensor_tensor(x5[j % 2][:, :, :], x5[j % 2][:, :, :], xn[:, :, 1:L1], ALU.add).then_inc(x5_ready, 1)

            def body(n, a=True, c=True):
                if a:
                    rstd(n + 1, ln1_var, ln1_rstd, ve1, rs1)
                    prev(n + 1, sx_ready, xprev, t["prev1"], xn)
                if c:
                    rstd(n - 1, ln2_var, ln2_rstd, ve2, rs2)
                if a:
                    add_x(n + 1, 0)
                    add_x(n + 1, 1)
                    add_x(n + 1, 2)
                if c:
                    prev(n - 1, sx2_ready, xprev2, t["prev0"], xn2)
                if a:
                    add_x(n + 1, 3)
                    add_x(n + 1, 4)
            rstd(0, ln1_var, ln1_rstd, ve1, rs1)
            prev(0, sx_ready, xprev, t["prev1"], xn)
            for j in range(5):
                add_x(0, j)
            body(0, c=False)
            with pool.Fori(1, CHUNKS - 1) as n:
                body(n)
            body(CHUNKS - 1, a=False)
            rstd(CHUNKS - 1, ln2_var, ln2_rstd, ve2, rs2)
            prev(CHUNKS - 1, sx2_ready, xprev2, t["prev0"], xn2)

        @block.tensor
        def _(pe):
            def a_bank(n, name):
                g = A_ORDER.index(name)
                same = [i for i in range(NA) if i % 3 == g % 3]
                at = same.index(g)
                s, i, count = A_READ[A_ORDER[same[at - 1]]]
                wait(pe, s, (n if at else n - 1) * count + i)
                return abank[g % 3]

            def c_bank(n, name):
                g = C_ORDER.index(name)
                s, i, count = C_READ[C_ORDER[g - 2]]
                if s is y_mid:
                    pe.wait_ge(s, n * count + i)
                else:
                    pe.wait_ge(s, n * count + i)
                return cbank[g % 2]

            def turn(src, bank_of, n, c):
                bank = bank_of(n, f"T{c}")
                for m in range(TILES):
                    mm = nc.tensor.transpose(bank[:, P * m:P * m + P], src[:, E * m + P * c:E * m + P * c + P], ident)
                return mm

            def project(bank, weight, src, o):
                for c in range(EC):
                    mm = nc.tensor.matmul(bank[:, :], wsq[:, weight, c, P * o:P * o + P], src(c), start=(c == 0), stop=(c == EC - 1))
                return mm

            def a_turn(n):
                pe.wait_ge(zn_ready, n * TILES + TILES)
                for c in range(EC):
                    turn(zn, a_bank, n, c).then_inc(a_done, 1)

            def a_mix(n):
                pe.wait_ge(xm_ready, n * 2 + 2)
                for name, lo, hi in (("m0", 0, P), ("m1", P, P + MIX)):
                    bank = a_bank(n, name)
                    for c in range(EC):
                        mm = nc.tensor.matmul(bank[0:hi - lo, :], t["w1"][:, c, lo:hi], xm[:, TOK * c:TOK * c + TOK],
                                              start=(c == 0), stop=(c == EC - 1))
                    mm.then_inc(a_done, 1)

            def a_mod(n, j):
                i = MIX_OF[j]
                pe.wait_ge(mix_tanh, n * 2 + (2 if i == 4 else 1))
                for c, name in enumerate((f"w{j}a", f"w{j}b")):
                    bank = a_bank(n, name)
                    if i < 4:
                        lhs, rhs = t["w2"][MIX * i:MIX * i + MIX, P * c:P * c + P], t1[MIX * i:MIX * i + MIX, :]
                    else:
                        lhs, rhs = low_w[0:MIX, P * c:P * c + P], low_t[0:MIX, :]
                    nc.tensor.matmul(bank[:, :], lhs, rhs, start=True, stop=True).then_inc(a_done, 1)

            def x5_half(j):
                return lambda c: x5[j % 2][:, NB * c:NB * c + NB, :].rearrange("p b t -> p (b t)")

            def a_dec1(n):
                pe.wait_ge(x5_ready, n * 5 + 1)
                bank = a_bank(n, "dec1")
                for c in range(EC):
                    mm = nc.tensor.matmul(bank[DEC:2 * DEC, :], t["dw1"][:, c, :], x5_half(0)(c), start=(c == 0), stop=(c == EC - 1))
                mm.then_inc(a_done, 1)

            def a_dec2(n):
                pe.wait_ge(dec_tanh, n + 1)
                for c, name in enumerate(("dec2a", "dec2b")):
                    nc.tensor.matmul(a_bank(n, name)[:, :], low_w[DEC:2 * DEC, P * c:P * c + P], low_t[DEC:2 * DEC, :],
                                     start=True, stop=True).then_inc(a_done, 1)

            def a_proj(n, j, letter, weight):
                pe.wait_ge(x5_ready, n * 5 + j + 1)
                for o in range(EC):
                    project(a_bank(n, f"{letter}{o}"), weight, x5_half(j), o).then_inc(a_done, 1)

            def b_head_sum(n, h):
                pe.wait_ge(ruk_ready, n * 2 + h + 1)
                wait(pe, bonus_ready, n * 2 + h)
                nc.tensor.matmul(sbank[:, :], ones_head, bon[h][:, :], start=True, stop=True).then_inc(head_sum, 1)

            def b_reduce(n, h, q):
                pe.wait_ge(prod_ready, n * 4 + 2 * h + q + 1)
                if q == 0:
                    wait(pe, gn_scaled, n * 2 + h - 1)
                for i in range(4):
                    mm = nc.tensor.matmul(att[h][:, :], cst[:, C_PROD + 4 * q + i, :], vb[h][:, 4 * q + i, :],
                                          start=(q == 0 and i == 0), stop=False)
                mm.then_inc(prod_used, 1)

            def b_bonus(n, h):
                pe.wait_ge(bonus_ready, n * 2 + h + 1)
                nc.tensor.matmul(att[h][:, :], cst[:, C_SELF, :], bon[h][:, :], start=False, stop=True).then_inc(att_done, 1)

            def c_var(n):
                for h in range(2):
                    pe.wait_ge(att_sq, n * 2 + h + 1)
                    nc.tensor.matmul(c_bank(n, f"var{h}")[:, :], avg_head, sq[h][:, :], start=True, stop=True).then_inc(c_done, 1)

            def rows(n, name, lhs, weight):
                i = int(name[1])
                bank = c_bank(n, name)
                for m in range(2):
                    for c in range(EC):
                        lo = P * (2 * i + m)
                        mm = nc.tensor.matmul(bank[:, E * m:E * m + E], lhs(c)[:, lo:lo + P], wsq[:, weight, c, :],
                                              start=(c == 0), stop=(c == EC - 1))
                mm.then_inc(c_done, 1)

            def c_out(n):
                pe.wait_ge(ag_ready, n * 2 + 2)
                rows(n, "o0", lambda c: ag[:, c, :], WO)
                rows(n, "o1", lambda c: ag[:, c, :], WO)

            def c_turn(n):
                pe.wait_ge(zn2_ready, n * TILES + TILES)
                for c in range(EC):
                    turn(zn2, c_bank, n, c).then_inc(c_done, 1)

            def c_key(n):
                pe.wait_ge(xk_ready, n * 2 + 2)
                for o in range(EC):
                    project(c_bank(n, f"k{o}"), FK, lambda c: zn2[:, TOK * c:TOK * c + TOK], o).then_inc(c_done, 1)

            def c_recept(n):
                pe.wait_ge(xr_ready, n * 2 + 2)
                rows(n, "r0", lambda c: xrr[:, c, :], FR)
                rows(n, "r1", lambda c: xrr[:, c, :], FR)

            def c_value(n):
                pe.wait_ge(kk_ready, n * 2 + 2)
                rows(n, "v0", lambda c: kk[:, c, :], FV)
                rows(n, "v1", lambda c: kk[:, c, :], FV)

            def body(n, a=True, b=True, c=True):
                if c:
                    c_var(n - 1)
                if b:
                    b_head_sum(n, 0)
                if a:
                    a_turn(n + 1)
                if b:
                    b_head_sum(n, 1)
                    b_reduce(n, 0, 0)
                if c:
                    c_out(n - 1)
                if a:
                    a_mix(n + 1)
                    a_mod(n + 1, 0)
                if b:
                    b_reduce(n, 0, 1)
                    b_bonus(n, 0)
                if a:
                    a_mod(n + 1, 1)
                    a_dec1(n + 1)
                    a_mod(n + 1, 2)
                    a_dec2(n + 1)
                    a_proj(n + 1, 1, "v", WV)
                if c:
                    c_turn(n - 1)
                if a:
                    a_mod(n + 1, 3)
                    a_proj(n + 1, 2, "k", WK)
                    a_mod(n + 1, 4)
                if b:
                    b_reduce(n, 1, 0)
                if c:
                    c_key(n - 1)
                if a:
                    a_proj(n + 1, 3, "r", WR)
                if c:
                    c_recept(n - 1)
                if a:
                    a_proj(n + 1, 4, "g", WG)
                if c:
                    c_value(n - 1)
                if b:
                    b_reduce(n, 1, 1)
                    b_bonus(n, 1)

            body(-1, b=False, c=False)
            body(0, c=False)
            with pe.Fori(1, CHUNKS - 2, 2) as n:
                body(n)
                body(n + 1)
            body(CHUNKS - 1, a=False)
            body(CHUNKS, a=False, b=False)

        @block.scalar
        def _(act):
            def a_bias(n):
                act.wait_ge(x_in, n * 16 + 16)
                nc.scalar.activation(xr_in[:, :, :], xr_in[:, :, :], ACT.Identity, bias=t["bnb"][:, 0:1]).then_inc(x_biased, 1)

            def a_xn(n):
                wait(act, x5_ready, n * 5)
                for c in range(EC):
                    act.wait_ge(a_done, a_at(n, f"T{c}"))
                    nc.scalar.activation(xn[:, NB * c:NB * c + NB, 1:L1], bt(ab(f"T{c}")[:, :]), ACT.Identity,
                                         bias=col(LN1B, c), scale=col(LN1W, c)).then_inc(xn_ready, 1)

            def a_tanh(n):
                act.wait_ge(a_done, a_at(n, "m0"))
                nc.scalar.activation(t1[:, :], ab("m0")[:, :], ACT.Tanh).then_inc(mix_tanh, 1)
                act.wait_ge(a_done, a_at(n, "m1"))
                nc.scalar.activation(low_t[0:MIX, :], ab("m1")[0:MIX, :], ACT.Tanh).then_inc(mix_tanh, 1)

            def a_dec(n):
                act.wait_ge(a_done, a_at(n, "dec1"))
                nc.scalar.activation(low_t[DEC:2 * DEC, :], ab("dec1")[DEC:2 * DEC, :], ACT.Tanh).then_inc(dec_tanh, 1)

            def a_w(n, p):
                for h, name in enumerate(("dec2a", "dec2b")):
                    act.wait_ge(a_done, a_at(n, name))
                    nc.scalar.activation(w[p][h][:, :, 1:L1], bt(ab(name)[:, :]), ACT.Exp, bias=col(TDEC, h)).then_inc(dec_exp, 1)
                for h in range(2):
                    act.wait_ge(dec_exp, n * 2 + h + 1)
                    nc.scalar.activation(w[p][h][:, :, 1:L1], w[p][h][:, :, 1:L1], ACT.Exp, scale=-1.0).then_inc(w_ready, 1)

            def a_copy(n, letter, dst, sem_out):
                for h in range(2):
                    act.wait_ge(a_done, a_at(n, f"{letter}{h}"))
                    if letter == "v":
                        wait(act, bonus_ready, (n - 1) * 2 + h + 1)
                        wait(act, v_spread[h], n * 16 * S)
                    nc.scalar.activation(dst[h][:, :], ab(f"{letter}{h}")[:, :], ACT.Copy).then_inc(sem_out, 1)

            def a_gate(n, p):
                for h in range(2):
                    act.wait_ge(a_done, a_at(n, f"g{h}"))
                    nc.scalar.activation(gate[p][h][:, :], ab(f"g{h}")[:, :], ACT.Tanh, scale=0.5).then_inc(g_tanh, 1)

            def c_square(n):
                for h in range(2):
                    act.wait_ge(att_done, n * 2 + h + 1)
                    nc.scalar.activation(sq[h][:, :], att[h][:, :], ACT.Square).then_inc(att_sq, 1)

            def c_rstd(n):
                for h in range(2):
                    act.wait_ge(c_done, c_at(n, f"var{h}"))
                    nc.scalar.activation(sq[h][:, :], cb(f"var{h}")[:, :], ACT.Ln, bias=eps[:, 0:1]).then_inc(var_ln, 1)
                for h in range(2):
                    act.wait_ge(var_ln, n * 2 + h + 1)
                    nc.scalar.activation(sq[h][:, :], sq[h][:, :], ACT.Exp, scale=-0.5).then_inc(gn_rstd, 1)

            def c_xn2(n):
                for c in range(EC):
                    act.wait_ge(c_done, c_at(n, f"T{c}"))
                    nc.scalar.activation(xn2[:, NB * c:NB * c + NB, 1:L1], bt(cb(f"T{c}")[:, :]), ACT.Identity,
                                         bias=col(LN2B, c), scale=col(LN2W, c)).then_inc(xn2_ready, 1)

            def c_kk(n):
                for c in range(EC):
                    act.wait_ge(c_done, c_at(n, f"k{c}"))
                    nc.scalar.activation(kk[:, c, :], cb(f"k{c}")[:, :], ACT.Relu).then_inc(relu_ready, 1)
                for c in range(EC):
                    act.wait_ge(relu_ready, n * 2 + c + 1)
                    nc.scalar.activation(kk[:, c, :], kk[:, c, :], ACT.Square).then_inc(kk_ready, 1)

            def c_rr(n):
                for i in range(2):
                    act.wait_ge(c_done, c_at(n, f"r{i}"))
                    nc.scalar.activation(rr[:, 2 * i:2 * i + 2, :], cb(f"r{i}")[:, :].rearrange("p (m f) -> p m f", m=2),
                                         ACT.Tanh, scale=0.5).then_inc(rr_ready, 1)

            def body(n, p, a=True, c=True):
                q = 1 - p
                if a:
                    a_bias(n + 1)
                if c:
                    c_square(n - 1)
                    c_rstd(n - 1)
                if a:
                    a_xn(n + 1)
                    a_tanh(n + 1)
                    a_dec(n + 1)
                    a_w(n + 1, q)
                    a_copy(n + 1, "v", v, v_ready)
                if c:
                    c_xn2(n - 1)
                if a:
                    a_copy(n + 1, "k", k[q], k_ready)
                if c:
                    c_kk(n - 1)
                if a:
                    a_copy(n + 1, "r", r[q], r_ready)
                if c:
                    c_rr(n - 1)
                if a:
                    a_gate(n + 1, q)


            act.wait_ge(init_done, 5)
            body(-1, 1, c=False)
            body(0, 0, c=False)
            with act.Fori(1, CHUNKS - 2, 2) as n:
                body(n, 1)
                body(n + 1, 0)
            body(CHUNKS - 1, (CHUNKS - 1) % 2, a=False)
            body(CHUNKS, CHUNKS % 2, a=False)

        @block.vector
        def _(dve):
            def moments(n, src_sem, src_at, stb, mvb, veb, s_st, s_mv, s_var):
                wait_apart(nc, dve, src_sem, src_at, eps[:, 1:2])
                for m in range(TILES):
                    nc.vector.bn_stats(stb[:, m, :], wyz[:, bass.ds(n * TILES + m, 1), :].rearrange("p a f -> p (a f)")).then_inc(s_st, 1)
                wait_apart(nc, dve, s_st, n * TILES + TILES, eps[:, 1:2])
                for m in range(TILES):
                    nc.vector.bn_aggr(mvb[:, m, :], stb[:, m, :]).then_inc(s_mv, 1)
                dve.wait_ge(s_mv, n * TILES + TILES)
                nc.vector.tensor_scalar(veb[:, :], mvb[:, :, 1], EPS, None, ALU.add).then_inc(s_var, 1)

            def normalise(n, s_rstd, mvb, rsb, dst, s_out):
                dve.wait_ge(s_rstd, n + 1)
                for m in range(TILES):
                    nc.vector.tensor_scalar(dst[:, E * m:E * m + E], wyz[:, bass.ds(n * TILES + m, 1), :].rearrange("p a f -> p (a f)"),
                                            mvb[:, m, 0:1], rsb[:, m:m + 1], ALU.subtract, ALU.mult).then_inc(s_out, 1)

            def a_z(n):
                dve.wait_ge(x_biased, n + 1)
                z = wyz[:, bass.ds(n * TILES, TILES), :]
                nc.vector.scalar_tensor_tensor(z, z, t["bna"][:, 0:1], xr_in[:, :, :], ALU.mult, ALU.add).then_inc(z_ready, 1)
                moments(n, z_ready, n + 1, st1b, mv1, ve1, st1, mv1_s, ln1_var)

            def a_norm(n):
                normalise(n, ln1_rstd, mv1, rs1, zn, zn_ready)

            def a_shift(n):
                dve.wait_ge(xn_ready, n * 2 + 2)
                dve.wait_ge(xprev, n * 2 + 2)
                nc.vector.tensor_tensor(sx[:, :, :], xn[:, :, 0:L], xn[:, :, 1:L1], ALU.subtract).then_inc(sx_ready, 1)
                dve.wait_ge(sx_ready, n + 1)
                for c in range(EC):
                    nc.vector.scalar_tensor_tensor(bt(xm[:, TOK * c:TOK * c + TOK]), sx[:, NB * c:NB * c + NB, :], col(MAAX, c),
                                                   xn[:, NB * c:NB * c + NB, 1:L1], ALU.mult, ALU.add).then_inc(xm_ready, 1)

            def a_mod(n, j):
                wait(dve, a_done, a_at(n, X5_READ_BY[j - 2]) if j >= 2 else a_at(n - 1, X5_READ_BY[4 - j]))
                for c, name in enumerate((f"w{j}a", f"w{j}b")):
                    dve.wait_ge(a_done, a_at(n, name))
                    nc.vector.scalar_tensor_tensor(x5[j % 2][:, NB * c:NB * c + NB, :], bt(ab(name)[:, :]), col(STK0 + MIX_OF[j], c),
                                                   sx[:, NB * c:NB * c + NB, :], ALU.add, ALU.mult).then_inc(mod_ready, 1)

            def a_gate(n, p):
                for h in range(2):
                    dve.wait_ge(g_tanh, n * 2 + h + 1)
                    nc.vector.scalar_tensor_tensor(gate[p][h][:, :], gate[p][h][:, :], 1.0, ab(f"g{h}")[:, :],
                                                   ALU.add, ALU.mult).then_inc(gate_ready, 1)

            def b_ruk(n, p):
                for h in range(2):
                    dve.wait_ge(k_ready, n * 2 + h + 1)
                    dve.wait_ge(r_ready, n * 2 + h + 1)
                    wait(dve, att_done, n * 2 + h - 1)
                    nc.vector.scalar_tensor_tensor(bon[h][:, :], r[p][h][:, :], col(BONUS, h), k[p][h][:, :], ALU.mult, ALU.mult).then_inc(ruk_ready, 1)

            def b_bonus(n, h):
                dve.wait_ge(head_sum, n * 2 + h + 1)
                dve.wait_ge(v_ready, n * 2 + h + 1)
                nc.vector.tensor_tensor(bon[h][:, :], sbank[:, :], v[h][:, :], ALU.mult).then_inc(bonus_ready, 1)

            def b_piece(n, p, h, q):
                if q == 0:
                    dve.wait_ge(v_spread[h], n * 16 * S + 16 * S)
                    dve.wait_ge(w_ready, n * 2 + h + 1)
                part = 2 * h + q

                def wide(ap):
                    return bt(ap).rearrange("p b (a t) -> p a b t", a=1).broadcast_to([P, 4, NB, L])

                src = vb[h][:, 4 * q:4 * q + 4, :].rearrange("p e (b t) -> p e b t", t=L)
                nc.vector.tensor_tensor(st[:, :, :, 1:L1], src, wide(k[p][h][:, :]), ALU.mult).then_inc(kv_ready, 1)
                nc.vector.tensor_copy(st[:, :, :, 0], t["s0"][:, h, 4 * q:4 * q + 4, bass.ds(n * NB, NB)]).then_inc(kv_ready, 1)
                dve.wait_ge(kv_ready, n * 8 + 2 * part + 2)
                for i in range(4):
                    row = st[:, i, :, :].rearrange("p b t -> p (b t)")
                    nc.vector.tensor_tensor_scan(row, w[p][h][:, :, :].rearrange("p b t -> p (b t)"), row, 0.0,
                                                 ALU.mult, ALU.add).then_inc(scanned, 1)
                dve.wait_ge(scanned, n * 16 + 4 * part + 4)
                nc.vector.tensor_tensor(src, st[:, :, :, 0:L], wide(r[p][h][:, :]), ALU.mult).then_inc(prod_ready, 1)

            def c_gn(n, p):
                for h in range(2):
                    dve.wait_ge(gn_rstd, n * 2 + h + 1)
                    nc.vector.scalar_tensor_tensor(ag[:, h, :], att[h][:, :], col(GNW, h), sq[h][:, :], ALU.mult, ALU.mult).then_inc(gn_scaled, 1)
                for h in range(2):
                    dve.wait_ge(gn_scaled, n * 2 + h + 1)
                    dve.wait_ge(gate_ready, n * 2 + h + 1)
                    nc.vector.scalar_tensor_tensor(ag[:, h, :], ag[:, h, :], col(GNB, h), gate[p][h][:, :], ALU.add, ALU.mult).then_inc(ag_ready, 1)

            def c_x1(n):
                for i in range(2):
                    dve.wait_ge(c_done, c_at(n, f"o{i}"))
                    z = wyz[:, bass.ds(n * TILES + 2 * i, 2), :]
                    nc.vector.scalar_tensor_tensor(z, cb(f"o{i}")[:, :].rearrange("p (m f) -> p m f", m=2), 0.5, z,
                                                   ALU.mult, ALU.add).then_inc(x1_ready, 1)
                moments(n, x1_ready, n * 2 + 2, st2b, mv2, ve2, st2, mv2_s, ln2_var)

            def c_norm(n):
                normalise(n, ln2_rstd, mv2, rs2, zn2, zn2_ready)

            def c_shift(n):
                dve.wait_ge(xn2_ready, n * 2 + 2)
                dve.wait_ge(xprev2, n * 2 + 2)
                dve.wait_ge(stored, n * 16 + 16)
                nc.vector.tensor_tensor(sx2[:, :, :], xn2[:, :, 0:L], xn2[:, :, 1:L1], ALU.subtract).then_inc(sx2_ready, 1)
                dve.wait_ge(sx2_ready, n + 1)
                for dst, v_, s_out in ((lambda c: zn2[:, TOK * c:TOK * c + TOK], FMK, xk_ready), (lambda c: xrr[:, c, :], FMR, xr_ready)):
                    for c in range(EC):
                        nc.vector.scalar_tensor_tensor(bt(dst(c)), sx2[:, NB * c:NB * c + NB, :], col(v_, c),
                                                       xn2[:, NB * c:NB * c + NB, 1:L1], ALU.mult, ALU.add).then_inc(s_out, 1)

            def c_final(n):
                for i in range(2):
                    dve.wait_ge(rr_ready, n * 2 + i + 1)
                    dve.wait_ge(c_done, c_at(n, f"v{i}"))
                    if i == 0:
                        dve.wait_ge(xr_ready, n * 2 + 2)
                    nc.vector.scalar_tensor_tensor(y[:, 2 * i:2 * i + 2, :], rr[:, 2 * i:2 * i + 2, :], 1.0,
                                                   cb(f"v{i}")[:, :].rearrange("p (m f) -> p m f", m=2), ALU.add, ALU.mult).then_inc(y_mid, 1)
                for i in range(2):
                    dve.wait_ge(y_mid, n * 2 + i + 3)
                    nc.vector.scalar_tensor_tensor(y[:, 2 * i:2 * i + 2, :], y[:, 2 * i:2 * i + 2, :], 0.5,
                                                   wyz[:, bass.ds(n * TILES + 2 * i, 2), :], ALU.mult, ALU.add).then_inc(out_ready, 1)

            def body(n, p, a=True, b=True, c=True):
                q = 1 - p
                if a:
                    a_z(n + 1)
                if b:
                    b_ruk(n, p)
                if a:
                    a_norm(n + 1)
                if b:
                    b_bonus(n, 0)
                    b_piece(n, p, 0, 0)
                if c:
                    c_gn(n - 1, q)
                if a:
                    a_shift(n + 1)
                if b:
                    b_bonus(n, 1)
                    b_piece(n, p, 0, 1)
                if c:
                    c_x1(n - 1)
                if a:
                    a_mod(n + 1, 0)
                    a_mod(n + 1, 1)
                if c:
                    c_norm(n - 1)
                if a:
                    a_mod(n + 1, 2)
                if b:
                    b_piece(n, p, 1, 0)
                if a:
                    a_mod(n + 1, 3)
                if c:
                    c_shift(n - 1)
                if a:
                    a_mod(n + 1, 4)
                if b:
                    b_piece(n, p, 1, 1)
                if a:
                    a_gate(n + 1, q)
                if c:
                    c_final(n - 1)

            nc.vector.memset(eps[:, 0:1], EPS).then_inc(init_done, 1)
            for p in range(2):
                for h in range(2):
                    nc.vector.memset(w[p][h][:, :, 0], 0.0).then_inc(init_done, 1)
            dve.sem_inc(y_mid, 2)
            dve.sem_inc(stored, 16)
            dve.wait_ge(init_done, 5)
            body(-1, 1, b=False, c=False)
            body(0, 0, c=False)
            with dve.Fori(1, CHUNKS - 2, 2) as n:
                body(n, 1)
                body(n + 1, 0)
            body(CHUNKS - 1, (CHUNKS - 1) % 2, a=False)
            body(CHUNKS, CHUNKS % 2, a=False, b=False)


def program(nc, d, out):
    ctx = ExitStack()
    with ctx:
        def sb(name, shape):
            return ctx.enter_context(nc.sbuf_tensor(name, shape, F32))

        def sem(name):
            return ctx.enter_context(nc.semaphore(name))

        t = {
            "wyz": sb("wyz", [P, PAIRS, T]),
            "stats": sb("stats", [P, PAIRS, 6]),
            "cst": sb("cst", [P, 13, P]),
            "vec": sb("vec", [P, 16, EC]),
            "bnv": sb("bnv", [P, 2]),
            "wsq": sb("wsq", [P, 8, EC, E]),
            "w1": sb("w1", [P, EC, 5 * MIX]),
            "w2": sb("w2", [P, E]),
            "low_w": sb("low_w", [P, E]),
            "dw1": sb("dw1", [P, EC, DEC]),
            "s0": sb("s0", [P, 2, S, B]),
            "prev1": sb("prev1", [P, EC, B]),
            "prev0": sb("prev0", [P, EC, B]),
            "bna": sb("bna", [P, 1]),
            "bnb": sb("bnb", [P, 1]),
            "mhalf": sb("mhalf", [P, TILES]),
            "s_late": sem("late_weights_in"),
        }
        attention(nc, sem, t, d)
        norm_params(nc, sem, t)
        rwkv(nc, sem, t, d, out)


def _constants():
    import numpy as np

    i = np.arange(P)
    same_head = (i[:, None] // S == i[None, :] // S).astype(np.float32)
    out = np.zeros((13, P, P), np.float32)
    for e in range(S):
        out[C_PROD + e] = same_head * ((i[None, :] % S == e).astype(np.float32) - 1.0 / S)
    out[C_SELF] = np.eye(P, dtype=np.float32) - same_head / S
    out[C_ONES] = same_head
    out[C_AVG] = same_head / S
    out[C_HALF] = (i[:, None] % C == i[None, :] % C).astype(np.float32) * 0.5
    out[C_ID] = np.eye(P, dtype=np.float32)
    return np.ascontiguousarray(out.transpose(1, 0, 2))


def kernel(**inputs):
    import numpy as np
    import concourse.bacc as bacc
    from concourse.bass_utils import run_bass_kernel_spmd

    a = {k: np.asarray(v) for k, v in inputs.items()}
    p1 = {k[len("L1_xattn_"):]: v for k, v in a.items() if k.startswith("L1_xattn_")}
    p0 = {k[len("L0_xattn_"):]: v for k, v in a.items() if k.startswith("L0_xattn_")}
    ctx = a["ctx_2048"]

    def halves(m):
        return m.reshape(EC, P, -1).transpose(1, 0, 2)

    vecs = [p1["ln1_w"], p1["ln1_b"], p1["ln2_w"], p1["ln2_b"], p1["maa_x"], *p1["maa_stack"], p1["time_decay"],
            p1["faaaa"].reshape(-1), p1["gn_w"], p1["gn_b"], p1["ffn_maa_k"], p1["ffn_maa_r"]]
    squares = [p1[n] for n in ("Wr", "Wk", "Wv", "Wg", "Wo", "ffn_Wk", "ffn_Wr", "ffn_Wv")]
    arrays = {
        "x": a["x"].reshape(PAIRS, P, T),
        "ctx": ctx.reshape(PAIRS, P, T),
        "cst": _constants(),
        "Wg": p0["Wg"], "WzT": p0["Wz"].T, "WthT": p0["Wtheta"].T, "WphT": p0["Wphi"].T,
        "bg": p0["bg"].reshape(CI, 1), "bz": p0["bz"].reshape(1, C),
        "bth": np.concatenate([p0["btheta"]] * 2).reshape(2 * CI, 1),
        "bph": np.concatenate([p0["bphi"]] * 2).reshape(2 * CI, 1),
        "bnv": np.stack([np.concatenate([p0[n]] * 2) for n in ("gamma", "beta")], axis=1),
        "vec": halves(np.stack(vecs, axis=1)).transpose(0, 2, 1),
        "wsq": np.stack([halves(m.T) for m in squares], axis=1),
        "w1": halves(p1["maa_w1"]),
        "w2": p1["maa_w2"].reshape(5 * MIX, E),
        "dw1": halves(p1["decay_w1"]),
        "dw2": p1["decay_w2"],
        "s0": ctx[:, 2:2 + S, :].reshape(B, 2, P, S).transpose(2, 1, 3, 0),
        "prev1": halves(ctx[:, 1, :].T),
        "prev0": halves(ctx[:, 0, :].T),
    }
    nc = bacc.Bacc("TRN2", target_bir_lowering=False, num_devices=1)
    feeds, d = {}, {}
    for name, m in arrays.items():
        m = np.ascontiguousarray(m)
        feeds[f"in_{name}"] = m
        d[name] = nc.dram_tensor(f"in_{name}", m.shape, mybir.dt.from_np(m.dtype), kind="ExternalInput").ap()
    out = nc.dram_tensor("out_0", (PAIRS, P, T), F32, kind="ExternalOutput").ap()
    program(nc, d, out)
    res = run_bass_kernel_spmd(nc, [feeds], core_ids=[0])
    return res.results[0]["out_0"].reshape(B, C, T)
```

```python
from contextlib import ExitStack

import concourse.bass as bass
from concourse import mybir

F32 = mybir.dt.float32
ALU = mybir.AluOpType
ACT = mybir.ActivationFunctionType
AX = mybir.AxisListType
P = 128
WARM_0, WARM_1, WARM_A, WARM_B, WARM_C, WARM_D = 8, 2, 2, 2, 6, 17

B, C, T, CI = 64, 64, 256, 32
L, E, H, S = C, T, 32, 8
EPS = 1e-5
PAIRS = B // 2
QUADS = B // 4
NB = 8
CHUNKS = B // NB
TOK = NB * L
TILES = TOK // P
EC = E // P
L1 = L + 1
MIX, DEC = 32, 64

(LN1W, LN1B, LN2W, LN2B, MAAX, STK0, TDEC, BONUS, GNW, GNB, FMK, FMR) = (0, 1, 2, 3, 4, 5, 10, 11, 12, 13, 14, 15)
WR, WK, WV, WG, WO, FK, FR, FV = range(8)
C_PROD, C_SELF, C_ONES, C_AVG, C_HALF, C_ID = 0, 8, 9, 10, 11, 12


def wait(eng, sem, value):
    if isinstance(value, int) and value <= 0:
        return
    eng.wait_ge(sem, value)


def wait_apart(nc, dve, sem, value, spare):
    dve.wait_ge(sem, value)
    if not isinstance(value, int):
        nc.vector.memset(spare, 0.0)


def keep_warm(nc, lhs, rhs, bank, count):
    for _ in range(count):
        nc.tensor.matmul(bank[:, 0:T], lhs, rhs, start=True, stop=True)


def attention(nc, sem, t, d):
    s_xin = [sem("pair_even_in"), sem("pair_odd_in")]
    s_w, s_cst = sem("weights_in"), sem("constants_in")
    s_zero, s_blank = sem("blockdiag_zeroed"), sem("blank_ready")
    s_bd = sem("blockdiag_in")
    s_wc, s_wcs = sem("gz_weight_done"), sem("gz_weight_ready")
    s_bgb = sem("bg_spread")
    s_proj, s_gz = sem("thetaphi_done"), sem("gz_done")
    s_thph, s_gzr = sem("thetaphi_ready"), sem("gz_ready")
    s_f, s_max, s_exp = sem("scores_done"), sem("negmax_ready"), sem("exp_ready")
    s_rec, s_scl = sem("rowsum_inverted"), sem("probs_scaled")
    s_t, s_pta, s_ptd = sem("probsT_done"), sem("probsT_even_ready"), sem("probsT_odd_ready")
    s_av, s_wy, s_bn = sem("av_done"), sem("wy_ready"), sem("stats_ready")
    wyz, stats, cst = t["wyz"], t["stats"], t["cst"]
    ident = cst[:, C_ID, :]


    def inside(pi):
        return not isinstance(pi, int) or 0 <= pi < PAIRS

    ctx = ExitStack()
    with ctx:
        def sb(name, shape):
            return ctx.enter_context(nc.sbuf_tensor(name, shape, F32))

        def pb(name):
            return ctx.enter_context(nc.psum_tensor(name, [P, 512], F32))

        x2 = [sb(f"x2_{p}", [P, T]) for p in range(2)]
        c2 = [sb(f"c2_{p}", [P, T]) for p in range(2)]
        bd_th, bd_ph, bd_gz = sb("bd_th", [P, 2 * CI]), sb("bd_ph", [P, 2 * CI]), sb("bd_gz", [P, 2 * C])
        bth, bph = sb("bth", [2 * CI, 1]), sb("bph", [P, 1])
        wg, wzT, bg, bz = sb("wg", [CI, C]), sb("wzT", [CI, C]), sb("bg", [CI, 1]), sb("bz", [1, C])
        bgb, ones = sb("bgb", [CI, P]), sb("ones", [CI, P])
        gzb = sb("gzb", [P, C])
        thph = [sb(f"thph{p}", [2 * CI, 2 * T]) for p in range(2)]
        gz = [sb(f"gz{p}", [P, 2, 2, C]) for p in range(2)]
        pr = [sb(f"probs{b}", [P, 2, T]) for b in range(4)]
        pT = [sb(f"probsT{b}", [P, 2, T]) for b in range(4)]
        nm = [sb(f"negmax{b}", [P, 2]) for b in range(4)]
        rs = [sb(f"rowsum{b}", [P, 2]) for b in range(4)]
        ri = [sb(f"rowinv{b}", [P, 3]) for b in range(4)]
        ps_proj, ps_gz = pb("ps_proj"), pb("ps_gz")
        ps_f, ps_t, ps_av = [pb("ps_f0"), pb("ps_f1")], [pb("ps_t0"), pb("ps_t1")], [pb("ps_av0"), pb("ps_av1")]
        block = ctx.enter_context(nc.Block())

        @block.sync
        def _(sp):
            def load_pair(pi, p):
                sp.dma_start(x2[p][:, :], d["x"][pi, :, :]).then_inc(s_xin[p], 16)
                sp.dma_start(c2[p][:, :], d["ctx"][pi, :, :]).then_inc(s_xin[p], 16)

            load_pair(0, 0)
            for dst, src in ((wg, d["Wg"]), (wzT, d["WzT"]), (bg, d["bg"]), (bz, d["bz"]), (bth, d["bth"]),
                             (bph[2 * CI:4 * CI, :], d["bph"])):
                sp.dma_start(dst[:, :], src).then_inc(s_w, 16)
            sp.wait_ge(s_zero, 3)
            for b in range(2):
                sp.dma_start(bd_th[C * b:C * b + C, CI * b:CI * b + CI], d["WthT"]).then_inc(s_bd, 16)
                sp.dma_start(bd_ph[C * b:C * b + C, CI * b:CI * b + CI], d["WphT"]).then_inc(s_bd, 16)
            sp.dma_start(ident, d["cst"][:, C_ID, :]).then_inc(s_cst, 16)
            load_pair(1, 1)
            with sp.Fori(1, QUADS) as q:
                for p in range(2):
                    sp.wait_ge(s_gz, q * 2 + p - 1)
                    sp.dma_start(x2[p][:, :], d["x"][bass.ds(q * 2 + p, 1)].rearrange("a p f -> p (a f)")).then_inc(s_xin[p], 16)
                    sp.dma_start(c2[p][:, :], d["ctx"][bass.ds(q * 2 + p, 1)].rearrange("a p f -> p (a f)")).then_inc(s_xin[p], 16)
            sp.dma_start(t["x_chunk"][:, :, :], d["x"][0:TILES].rearrange("a p f -> p a f")).then_inc(t["x_in"], 16)

        @block.gpsimd
        def _(pool):
            for m, value in ((ones, 1.0), (bd_th, 0.0), (bd_ph, 0.0), (bd_gz, 0.0)):
                nc.gpsimd.memset(m[:, :], value).then_inc(s_zero, 1)
            pool.wait_ge(s_xin[1], 64)
            for dst, src in ((t["cst"][:, 0:C_ID, :], d["cst"][:, 0:C_ID, :]), (t["vec"], d["vec"]), (t["bnv"], d["bnv"]), (t["wsq"], d["wsq"]), (t["w1"], d["w1"]),
                             (t["w2"], d["w2"][0:P, :]), (t["dw1"], d["dw1"]), (t["s0"], d["s0"]),
                             (t["prev1"], d["prev1"]), (t["prev0"], d["prev0"])):
                pool.dma_start(dst[(slice(None),) * len(dst.shape)], src).then_inc(t["s_late"], 16)
            pool.dma_start(t["low_w"][0:MIX, :], d["w2"][P:P + MIX, :]).then_inc(t["s_late"], 16)
            pool.dma_start(t["low_w"][DEC:2 * DEC, :], d["dw2"]).then_inc(t["s_late"], 16)

        @block.tensor
        def _(pe):
            def proj(pi, p):
                wait(pe, s_xin[p], (pi - p) * 16 + 32)
                wait(pe, s_thph, pi * 2)
                nc.tensor.matmul(ps_proj[0:2 * CI, 0:T], bd_th[:, :], x2[p][:, :], start=True, stop=True)
                nc.tensor.matmul(ps_proj[2 * CI:4 * CI, T:2 * T], bd_ph[:, :], c2[p][:, :], start=True, stop=True).then_inc(s_proj, 1)
                wait(pe, s_gzr, pi)
                for j in range(2):
                    mm = nc.tensor.matmul(ps_gz[:, P * j:P * j + P], x2[p][:, P * j:P * j + P], bd_gz[:, :], start=True, stop=True)
                mm.then_inc(s_gz, 1)

            def scores(pi, p, e):
                wait(pe, s_thph, pi * 2 + 2)
                wait(pe, s_exp, pi * 2 + e - 1)
                r = CI * e
                tp = thph[p]
                for i in range(2):
                    mm = nc.tensor.matmul(ps_f[e][:, T * i:T * i + T], tp[r:r + CI, T + P * i:T + P * i + P],
                                          tp[r:r + CI, 0:T], start=True, stop=True)
                mm.then_inc(s_f, 1)

            def transposes(pi, p, e):
                wait(pe, s_scl, (pi * 2 + e) * 2 + 2)
                wait(pe, (s_pta, s_ptd)[e], pi)
                for j in range(2):
                    for i in range(2):
                        mm = nc.tensor.transpose(ps_t[e][:, T * j + P * i:T * j + P * i + P],
                                                 pr[2 * p + e][:, i, P * j:P * j + P], ident)
                mm.then_inc(s_t, 1)

            def attend(pi, p, e):
                wait(pe, (s_pta, s_ptd)[e], pi + 1)
                wait(pe, s_gzr, pi + 1)
                if e == 0:
                    wait(pe, s_wy, pi - 1)
                r = C * e
                for j in range(2):
                    mm = nc.tensor.matmul(ps_av[p][r:r + C, 0:T], gz[p][:, j, e, :], pT[2 * p + e][:, j, :],
                                          start=(j == 0), stop=(j == 1))
                mm.then_inc(s_av, 1)

            def body(n, p):
                if inside(n - 2):
                    attend(n - 2, p, 1)
                if inside(n):
                    scores(n, p, 0)
                if inside(n - 1):
                    transposes(n - 1, 1 - p, 0)
                if inside(n):
                    scores(n, p, 1)
                if inside(n - 1):
                    transposes(n - 1, 1 - p, 1)
                if inside(n + 1):
                    proj(n + 1, 1 - p)
                if inside(n - 1):
                    attend(n - 1, 1 - p, 0)

            def warm(count):
                keep_warm(nc, wyz[:, 0, 0:P], wyz[:, 0, :], ps_av[1], count)

            pe.wait_ge(s_blank, 1)
            warm(WARM_0)
            pe.wait_ge(s_w, 16 * 6)
            pe.wait_ge(s_bgb, 1)
            pe.wait_ge(s_zero, 4)
            nc.tensor.matmul(ps_gz[0:C, 0:C], wg[:, :], wzT[:, :], start=True, stop=True)
            nc.tensor.matmul(ps_gz[C:2 * C, 0:C], wg[:, :], wzT[:, :], start=True, stop=True)
            nc.tensor.matmul(ps_proj[:, 0:C], bgb[:, :], wzT[:, :], start=True, stop=False)
            nc.tensor.matmul(ps_proj[:, 0:C], ones[0:1, :], bz[:, :], start=False, stop=True).then_inc(s_wc, 1)
            pe.wait_ge(s_wcs, 3)
            pe.wait_ge(s_bd, 64)
            warm(WARM_1)
            pe.wait_ge(s_wcs, 3)
            pe.wait_ge(s_bd, 64)
            for n in range(-1, 5):
                if n == 0:
                    pe.wait_ge(s_cst, 16)
                body(n, n % 2)
            with pe.Fori(5, PAIRS - 1, 2) as n:
                body(n, 1)
                body(n + 1, 0)
            for n in range(PAIRS - 1, PAIRS + 2):
                body(n, n % 2)

        @block.scalar
        def _(act):
            def exps(pi, p, e):
                wait(act, s_max, pi * 2 + e + 1)
                wait(act, s_t, pi * 2 + e - 3)
                b = 2 * p + e
                for i in range(2):
                    mm = nc.scalar.activation(pr[b][:, i, :], ps_f[e][:, T * i:T * i + T], ACT.Exp,
                                              bias=nm[b][:, i:i + 1], accum_out=rs[b][:, i:i + 1])
                mm.then_inc(s_exp, 1)

            def theta_phi(pi, p):
                wait(act, s_proj, pi + 1)
                wait(act, s_f, pi * 2 - 2)
                nc.scalar.activation(thph[p][:, 0:T], ps_proj[0:2 * CI, 0:T], ACT.Identity, bias=bth[:, 0:1]).then_inc(s_thph, 1)
                nc.scalar.activation(thph[p][:, T:2 * T], ps_proj[2 * CI:4 * CI, T:2 * T], ACT.Identity,
                                     bias=bph[2 * CI:4 * CI, 0:1]).then_inc(s_thph, 1)

            def probs_t(pi, p):
                wait(act, s_t, pi * 2 + 1)
                wait(act, s_av, pi * 2 - 3)
                nc.scalar.activation(pT[2 * p][:, :, :], ps_t[0][:, :].rearrange("p (j i) -> p j i", j=2), ACT.Copy).then_inc(s_pta, 1)

            def w_y(pi, p):
                wait(act, s_av, pi * 2 + 2)
                nc.scalar.activation(wyz[:, bass.ds(pi, 1), :], ps_av[p][:, 0:T].rearrange("p (a f) -> p a f", a=1), ACT.Copy).then_inc(s_wy, 1)

            def body(n, p):
                if inside(n):
                    exps(n, p, 0)
                if inside(n + 1):
                    theta_phi(n + 1, 1 - p)
                if inside(n):
                    exps(n, p, 1)
                    probs_t(n, p)
                if inside(n - 1):
                    w_y(n - 1, 1 - p)

            act.wait_ge(s_wc, 1)
            nc.scalar.copy(bd_gz[0:C, 0:C], ps_gz[0:C, 0:C]).then_inc(s_wcs, 1)
            nc.scalar.copy(bd_gz[C:2 * C, C:2 * C], ps_gz[C:2 * C, 0:C]).then_inc(s_wcs, 1)
            nc.scalar.copy(gzb[:, :], ps_proj[:, 0:C]).then_inc(s_wcs, 1)
            for n in range(-1, 5):
                body(n, n % 2)
            with act.Fori(5, PAIRS - 1, 2) as n:
                body(n, 1)
                body(n + 1, 0)
            for n in range(PAIRS - 1, PAIRS + 1):
                body(n, n % 2)

        @block.vector
        def _(dve):
            def negmax(pi, p, e):
                wait(dve, s_f, pi * 2 + e + 1)
                nc.vector.tensor_reduce(nm[2 * p + e][:, :], ps_f[e][:, :].rearrange("p (i j) -> p i j", i=2), AX.X, ALU.max,
                                        negate=True).then_inc(s_max, 1)

            def scale(pi, p, e):
                b = 2 * p + e
                wait(dve, s_exp, pi * 2 + e + 1)
                nc.vector.reciprocal(ri[b][:, 0:2], rs[b][:, :]).then_inc(s_rec, 1)
                wait(dve, s_rec, pi * 2 + e + 1)
                for i in range(2):
                    nc.vector.tensor_scalar(pr[b][:, i, :], pr[b][:, i, :], ri[b][:, i:i + 1], None, ALU.mult).then_inc(s_scl, 1)

            def probs_t(pi, p):
                wait(dve, s_t, pi * 2 + 2)
                wait(dve, s_av, pi * 2 - 2)
                nc.vector.tensor_copy(pT[2 * p + 1][:, :, :], ps_t[1][:, :].rearrange("p (j i) -> p j i", j=2)).then_inc(s_ptd, 1)

            def gz_out(pi, p):
                wait(dve, s_gz, pi + 1)
                wait(dve, s_av, pi * 2 - 2)
                nc.vector.tensor_tensor(gz[p][:, :, :, :].rearrange("p j b c -> p (j b) c"),
                                        ps_gz[:, 0:T].rearrange("p (j c) -> p j c", c=C),
                                        gzb[:, :].rearrange("p (a c) -> p a c", a=1).broadcast_to([P, 4, C]), ALU.add).then_inc(s_gzr, 1)

            def statistics(pi, p):
                wait_apart(nc, dve, s_wy, pi + 1, ri[0][:, 2:3])
                nc.vector.bn_stats(stats[:, bass.ds(pi, 1), :].rearrange("p a s -> p (a s)"),
                                   wyz[:, bass.ds(pi, 1), :].rearrange("p a f -> p (a f)")).then_inc(s_bn, 1)

            def body(n, p):
                if inside(n - 2):
                    statistics(n - 2, p)
                if inside(n + 1):
                    negmax(n + 1, 1 - p, 1)
                if inside(n):
                    probs_t(n, p)
                if inside(n + 1):
                    scale(n + 1, 1 - p, 0)
                if inside(n + 2):
                    gz_out(n + 2, p)
                if inside(n + 1):
                    scale(n + 1, 1 - p, 1)
                if inside(n + 2):
                    negmax(n + 2, p, 0)

            nc.vector.memset(wyz[:, 0, :], 0.0).then_inc(s_blank, 1)
            dve.wait_ge(s_w, 16 * 6)
            dve.wait_ge(s_zero, 4)
            nc.vector.tensor_scalar(bgb[:, :], ones[:, :], bg[:, 0:1], None, ALU.mult).then_inc(s_bgb, 1)
            dve.wait_ge(s_wcs, 3)
            for n in range(-2, 6):
                body(n, n % 2)
            with dve.Fori(6, PAIRS - 2, 2) as n:
                body(n, 0)
                body(n + 1, 1)
            for n in range(PAIRS - 2, PAIRS + 2):
                body(n, n % 2)

            dve.wait_ge(s_bn, PAIRS)


def norm_params(nc, sem, t):
    s_loc, s_mean, s_dev, s_var = sem("local_moments"), sem("mean_done"), sem("deviation_ready"), sem("var_done")
    s_ve, s_pw, s_par, s_half = sem("var_eps_ready"), sem("bn_rstd_ready"), sem("bn_params_ready"), sem("pow_exponent_ready")
    ctx = ExitStack()
    with ctx:
        mv = ctx.enter_context(nc.sbuf_tensor("mv", [P, 8], F32))
        ps = ctx.enter_context(nc.psum_tensor("ps_bn", [P, 512], F32))
        ps2 = ctx.enter_context(nc.psum_tensor("ps_bn2", [P, 512], F32))
        spare = ctx.enter_context(nc.psum_tensor("ps_spare", [P, 512], F32))
        block = ctx.enter_context(nc.Block())
        half = t["cst"][:, C_HALF, :]

        def warm(count):
            keep_warm(nc, t["cst"][:, C_ID, :], t["cst"][:, 0:2, :].rearrange("p a b -> p (a b)"), spare, count)

        @block.tensor
        def _(pe):
            pe.wait_ge(t["s_late"], 16 * 12)
            warm(WARM_A)
            pe.wait_ge(s_loc, 1)
            nc.tensor.matmul(ps[:, 0:2], half, mv[:, 0:2], start=True, stop=True).then_inc(s_mean, 1)
            warm(WARM_B)
            pe.wait_ge(s_dev, 4)
            nc.tensor.matmul(ps2[:, 0:2], half, mv[:, 4:6], start=True, stop=True).then_inc(s_var, 1)
            warm(WARM_C)

        @block.gpsimd
        def _(pool):
            nc.gpsimd.memset(t["mhalf"][:, :], -0.5).then_inc(s_half, 1)
            pool.wait_ge(s_half, 1)
            pool.wait_ge(s_ve, 1)
            nc.gpsimd.tensor_tensor(mv[:, 6:7], mv[:, 6:7], t["mhalf"][:, 0:1], ALU.pow).then_inc(s_pw, 1)

        @block.vector
        def _(dve):
            nc.vector.bn_aggr(mv[:, 0:2], t["stats"][:, :, :].rearrange("p a s -> p (a s)")).then_inc(s_loc, 1)
            dve.wait_ge(s_mean, 1)
            nc.vector.tensor_copy(mv[:, 2:3], ps[:, 0:1]).then_inc(s_dev, 1)
            dve.wait_ge(s_dev, 1)
            nc.vector.tensor_tensor(mv[:, 3:4], mv[:, 0:1], mv[:, 2:3], ALU.subtract).then_inc(s_dev, 1)
            dve.wait_ge(s_dev, 2)
            nc.vector.tensor_tensor(mv[:, 5:6], mv[:, 3:4], mv[:, 3:4], ALU.mult).then_inc(s_dev, 1)
            dve.wait_ge(s_dev, 3)
            nc.vector.tensor_tensor(mv[:, 4:5], mv[:, 1:2], mv[:, 5:6], ALU.add).then_inc(s_dev, 1)
            dve.wait_ge(s_var, 1)
            nc.vector.tensor_scalar(mv[:, 6:7], ps2[:, 0:1], EPS, None, ALU.add).then_inc(s_ve, 1)
            dve.wait_ge(s_pw, 1)
            dve.wait_ge(t["s_late"], 16 * 12)
            nc.vector.tensor_tensor(t["bna"][:, :], mv[:, 6:7], t["bnv"][:, 0:1], ALU.mult).then_inc(s_par, 1)
            dve.wait_ge(s_par, 1)
            nc.vector.tensor_tensor(mv[:, 7:8], mv[:, 2:3], t["bna"][:, :], ALU.mult).then_inc(s_par, 1)
            dve.wait_ge(s_par, 2)
            nc.vector.tensor_tensor(t["bnb"][:, :], t["bnv"][:, 1:2], mv[:, 7:8], ALU.subtract).then_inc(s_par, 1)
            dve.wait_ge(s_par, 3)


def rwkv(nc, sem, t, d, out):
    wyz, cst, vec, wsq, low_w, xr_in = t["wyz"], t["cst"], t["vec"], t["wsq"], t["low_w"], t["x_chunk"]
    ident, ones_head, avg_head = cst[:, C_ID, :], cst[:, C_ONES, :], cst[:, C_AVG, :]

    def col(v, c):
        return vec[:, v, c:c + 1]

    x_in, x_biased, z_ready = t["x_in"], sem("x_biased"), sem("z_ready")
    st1, mv1_s, ln1_var, ln1_rstd, zn_ready = sem("ln1_stats"), sem("ln1_moments"), sem("ln1_var"), sem("ln1_rstd"), sem("zn_ready")
    xn_ready, xprev, sx_ready, xm_ready = sem("xn_ready"), sem("xprev_ready"), sem("sx_ready"), sem("xm_ready")
    mix_tanh, mod_ready, x5_ready = sem("mix_tanh"), sem("modulated"), sem("x5_ready")
    dec_tanh, dec_exp, w_ready = sem("decay_tanh"), sem("decay_exp"), sem("w_ready")
    v_ready, k_ready, r_ready, g_tanh, gate_ready = sem("v_ready"), sem("k_ready"), sem("r_ready"), sem("gate_tanh"), sem("gate_ready")
    a_done = sem("a_matmuls_done")
    v_spread = [sem("v_spread_0"), sem("v_spread_1")]
    ruk_ready, head_sum, bonus_ready = sem("ruk_ready"), sem("head_sum_done"), sem("bonus_ready")
    kv_ready, scanned, prod_ready, prod_used, att_done = sem("kv_ready"), sem("scanned"), sem("prod_ready"), sem("prod_used"), sem("att_done")
    att_sq, var_ln, gn_rstd, gn_scaled, ag_ready = sem("att_squared"), sem("var_ln"), sem("gn_rstd"), sem("att_scaled"), sem("att_gated")
    x1_ready, st2, mv2_s, ln2_var, ln2_rstd, zn2_ready = sem("x1_ready"), sem("ln2_stats"), sem("ln2_moments"), sem("ln2_var"), sem("ln2_rstd"), sem("zn2_ready")
    xn2_ready, xprev2, sx2_ready, xk_ready, xr_ready = sem("xn2_ready"), sem("xprev2_ready"), sem("sx2_ready"), sem("xk_ready"), sem("xr_ready")
    relu_ready, kk_ready, rr_ready, y_mid, out_ready, stored = sem("relu_ready"), sem("kk_ready"), sem("rr_ready"), sem("y_mid"), sem("out_ready"), sem("out_stored")
    c_done = sem("c_matmuls_done")
    init_done = sem("init_done")

    A_ORDER = ["g0", "g1", "T0", "T1", "m0", "m1", "w0a", "w0b", "w1a", "w1b", "w2a", "w2b", "dec1", "dec2a", "dec2b",
               "v0", "v1", "w3a", "w3b", "k0", "k1", "w4a", "w4b", "r0", "r1"]
    A_READ = {"T0": (xn_ready, 1, 2), "T1": (xn_ready, 2, 2), "m0": (mix_tanh, 1, 2), "m1": (mix_tanh, 2, 2),
              "dec1": (dec_tanh, 1, 1), "dec2a": (dec_exp, 1, 2), "dec2b": (dec_exp, 2, 2),
              "v0": (v_ready, 1, 2), "v1": (v_ready, 2, 2), "k0": (k_ready, 1, 2), "k1": (k_ready, 2, 2),
              "r0": (r_ready, 1, 2), "r1": (r_ready, 2, 2), "g0": (gate_ready, 1, 2), "g1": (gate_ready, 2, 2)}
    for j in range(5):
        A_READ[f"w{j}a"], A_READ[f"w{j}b"] = (mod_ready, 2 * j + 1, 10), (mod_ready, 2 * j + 2, 10)
    NA = len(A_ORDER)
    C_ORDER = ["var0", "var1", "o0", "o1", "T0", "T1", "k0", "k1", "r0", "r1", "v0", "v1"]
    C_READ = {"var0": (var_ln, 1, 2), "var1": (var_ln, 2, 2), "o0": (x1_ready, 1, 2), "o1": (x1_ready, 2, 2),
              "T0": (xn2_ready, 1, 2), "T1": (xn2_ready, 2, 2), "k0": (relu_ready, 1, 2), "k1": (relu_ready, 2, 2),
              "r0": (rr_ready, 1, 2), "r1": (rr_ready, 2, 2), "v0": (y_mid, 1, 2), "v1": (y_mid, 2, 2)}
    NC = len(C_ORDER)
    MIX_OF = [1, 2, 0, 3, 4]
    X5_READ_BY = ["dec1", "v1", "k1", "r1", "g1"]

    ctx = ExitStack()
    with ctx:
        def sb(name, shape):
            return ctx.enter_context(nc.sbuf_tensor(name, shape, F32))

        def pb(name):
            return ctx.enter_context(nc.psum_tensor(name, [P, 512], F32))

        eps = sb("eps", [P, 2])
        zn = sb("zn", [P, TILES * E])
        xm = zn
        zn2 = sb("zn2", [P, TILES * E])
        st1b, mv1, ve1, rs1 = sb("st1", [P, TILES, 6]), sb("mv1", [P, TILES, 2]), sb("ve1", [P, TILES]), sb("rs1", [P, TILES])
        st2b, mv2, ve2, rs2 = sb("st2", [P, TILES, 6]), sb("mv2", [P, TILES, 2]), sb("ve2", [P, TILES]), sb("rs2", [P, TILES])
        xn, xn2 = sb("xn", [P, EC * NB, L1]), sb("xn2", [P, EC * NB, L1])
        sx = sb("sx", [P, EC * NB, L])
        sx2 = sb("sx2", [P, EC * NB, L])
        y = sx2[:, :, :].rearrange("p a b -> p (a b)").rearrange("p (m f) -> p m f", m=TILES)
        t1 = sb("mix_t", [P, TOK])
        low_t = sb("low_t", [P, TOK])
        x5 = [sb(f"x5_{i}", [P, EC * NB, L]) for i in range(2)]
        w = [[sb(f"w_{p}{h}", [P, NB, L1]) for h in range(2)] for p in range(2)]
        r = [[sb(f"r_{p}{h}", [P, TOK]) for h in range(2)] for p in range(2)]
        k = [[sb(f"k_{p}{h}", [P, TOK]) for h in range(2)] for p in range(2)]
        v = [sb(f"v_{h}", [P, TOK]) for h in range(2)]
        gate = [[sb(f"gate_{p}{h}", [P, TOK]) for h in range(2)] for p in range(2)]
        vb = [sb(f"vb_{h}", [P, S, TOK]) for h in range(2)]
        st = sb("state", [P, 4, NB, L1])
        bon = [sb(f"bonus_{h}", [P, TOK]) for h in range(2)]
        sq = [sb(f"sq_{h}", [P, TOK]) for h in range(2)]
        ag = sb("ag", [P, 2, TOK])
        rr = ag[:, :, :].rearrange("p h t -> p (h t)").rearrange("p (m f) -> p m f", m=TILES)
        xrr = sb("xr", [P, EC, TOK])
        kk = sb("kk", [P, EC, TOK])
        abank = [pb(f"ps_a{i}") for i in range(3)]
        cbank = [pb(f"ps_c{i}") for i in range(2)]
        sbank = pb("ps_headsum")
        att = [pb(f"ps_att{h}") for h in range(2)]
        block = ctx.enter_context(nc.Block())

        def bt(ap):
            return ap.rearrange("p (b t) -> p b t", t=L)

        def ab(name):
            return abank[A_ORDER.index(name) % 3]

        def cb(name):
            return cbank[C_ORDER.index(name) % 2]

        def a_body(n, name):
            return n if name in ("g0", "g1") else n - 1

        def a_at(n, name):
            return (a_body(n, name) + 1) * NA - 2 + A_ORDER.index(name) + 1

        def c_at(n, name):
            return n * NC + C_ORDER.index(name) + 1

        @block.sync
        def _(sp):
            def load_x(n):
                wait(sp, z_ready, n)
                sp.dma_start(xr_in[:, :, :], d["x"][bass.ds(n * TILES, TILES)].rearrange("a p f -> p a f")).then_inc(x_in, 16)

            def spread_v(n, h):
                sp.wait_ge(v_ready, n * 2 + h + 1)
                wait(sp, prod_used, n * 4 + 2 * h - 2)
                for i in range(S):
                    sp.dma_start(vb[h][i:P:S, :, :], v[h][:, :]).then_inc(v_spread[h], 16)

            def store(n):
                sp.wait_ge(out_ready, n * 2 + 2)
                sp.dma_start(out[bass.ds(n * TILES, TILES)].rearrange("a p f -> p a f"), y).then_inc(stored, 16)

            def body(n, c=True, a=True, x=True):
                if x:
                    load_x(n + 2)
                if a:
                    spread_v(n + 1, 0)
                if c:
                    store(n - 1)
                if a:
                    spread_v(n + 1, 1)

            load_x(1)
            spread_v(0, 0)
            spread_v(0, 1)
            body(0, c=False)
            with sp.Fori(1, CHUNKS - 2) as n:
                body(n)
            body(CHUNKS - 2, x=False)
            body(CHUNKS - 1, a=False, x=False)
            store(CHUNKS - 1)
            sp.wait_ge(stored, 16 * CHUNKS + 16)

        @block.gpsimd
        def _(pool):
            def rstd(n, var_sem, sem_out, src, dst):
                pool.wait_ge(var_sem, n + 1)
                nc.gpsimd.tensor_tensor(dst[:, :], src[:, :], t["mhalf"][:, :], ALU.pow).then_inc(sem_out, 1)

            def prev(n, shift_sem, sem_out, src, dst):
                wait(pool, shift_sem, n)
                for c in range(EC):
                    nc.gpsimd.tensor_copy(dst[:, NB * c:NB * c + NB, 0], src[:, c, bass.ds(n * NB, NB)]).then_inc(sem_out, 1)

            def add_x(n, j):
                pool.wait_ge(mod_ready, n * 10 + 2 * j + 2)
                nc.gpsimd.tensor_tensor(x5[j % 2][:, :, :], x5[j % 2][:, :, :], xn[:, :, 1:L1], ALU.add).then_inc(x5_ready, 1)

            def body(n, a=True, c=True):
                if a:
                    prev(n + 1, sx_ready, xprev, t["prev1"], xn)
                    rstd(n + 1, ln1_var, ln1_rstd, ve1, rs1)
                if c:
                    prev(n - 1, sx2_ready, xprev2, t["prev0"], xn2)
                if a:
                    add_x(n + 1, 0)
                if c:
                    rstd(n - 1, ln2_var, ln2_rstd, ve2, rs2)
                if a:
                    add_x(n + 1, 1)
                    add_x(n + 1, 2)
                    add_x(n + 1, 3)
                    add_x(n + 1, 4)

            rstd(0, ln1_var, ln1_rstd, ve1, rs1)
            prev(0, sx_ready, xprev, t["prev1"], xn)
            rstd(1, ln1_var, ln1_rstd, ve1, rs1)
            add_x(0, 0)
            add_x(0, 1)
            add_x(0, 2)
            add_x(0, 3)
            add_x(0, 4)
            prev(1, sx_ready, xprev, t["prev1"], xn)
            add_x(1, 0)
            add_x(1, 1)
            add_x(1, 2)
            add_x(1, 3)
            add_x(1, 4)
            with pool.Fori(1, CHUNKS - 1) as n:
                body(n)
            prev(CHUNKS - 2, sx2_ready, xprev2, t["prev0"], xn2)
            rstd(CHUNKS - 2, ln2_var, ln2_rstd, ve2, rs2)
            rstd(CHUNKS - 1, ln2_var, ln2_rstd, ve2, rs2)
            prev(CHUNKS - 1, sx2_ready, xprev2, t["prev0"], xn2)

        @block.tensor
        def _(pe):
            def warm(count):
                keep_warm(nc, ident, cst[:, 0:2, :].rearrange("p a b -> p (a b)"), sbank, count)

            def a_bank(n, name):
                g = A_ORDER.index(name)
                same = [i for i in range(NA) if i % 3 == g % 3]
                at = same.index(g)
                before = A_ORDER[same[at - 1]]
                s, i, count = A_READ[before]
                in_body = a_body(n, name) if at else a_body(n, name) - 1
                wait(pe, s, (in_body if before in ("g0", "g1") else in_body + 1) * count + i)
                return abank[g % 3]

            def c_bank(n, name):
                g = C_ORDER.index(name)
                s, i, count = C_READ[C_ORDER[g - 2]]
                if s is y_mid:
                    pe.wait_ge(s, n * count + i)
                else:
                    pe.wait_ge(s, n * count + i)
                return cbank[g % 2]

            def turn(src, bank_of, n, c):
                bank = bank_of(n, f"T{c}")
                for m in range(TILES):
                    mm = nc.tensor.transpose(bank[:, P * m:P * m + P], src[:, E * m + P * c:E * m + P * c + P], ident)
                return mm

            def project(bank, weight, src, o):
                for c in range(EC):
                    mm = nc.tensor.matmul(bank[:, :], wsq[:, weight, c, P * o:P * o + P], src(c), start=(c == 0), stop=(c == EC - 1))
                return mm

            def a_turn(n):
                pe.wait_ge(zn_ready, n * TILES + TILES)
                for c in range(EC):
                    turn(zn, a_bank, n, c).then_inc(a_done, 1)

            def a_mix(n):
                pe.wait_ge(xm_ready, n * 2 + 2)
                for name, lo, hi in (("m0", 0, P), ("m1", P, P + MIX)):
                    bank = a_bank(n, name)
                    for c in range(EC):
                        mm = nc.tensor.matmul(bank[0:hi - lo, :], t["w1"][:, c, lo:hi], xm[:, TOK * c:TOK * c + TOK],
                                              start=(c == 0), stop=(c == EC - 1))
                    mm.then_inc(a_done, 1)

            def a_mod(n, j):
                i = MIX_OF[j]
                pe.wait_ge(mix_tanh, n * 2 + (2 if i == 4 else 1))
                for c, name in enumerate((f"w{j}a", f"w{j}b")):
                    bank = a_bank(n, name)
                    if i < 4:
                        lhs, rhs = t["w2"][MIX * i:MIX * i + MIX, P * c:P * c + P], t1[MIX * i:MIX * i + MIX, :]
                    else:
                        lhs, rhs = low_w[0:MIX, P * c:P * c + P], low_t[0:MIX, :]
                    nc.tensor.matmul(bank[:, :], lhs, rhs, start=True, stop=True).then_inc(a_done, 1)

            def x5_half(j):
                return lambda c: x5[j % 2][:, NB * c:NB * c + NB, :].rearrange("p b t -> p (b t)")

            def a_dec1(n):
                pe.wait_ge(x5_ready, n * 5 + 1)
                bank = a_bank(n, "dec1")
                for c in range(EC):
                    mm = nc.tensor.matmul(bank[DEC:2 * DEC, :], t["dw1"][:, c, :], x5_half(0)(c), start=(c == 0), stop=(c == EC - 1))
                mm.then_inc(a_done, 1)

            def a_dec2(n):
                pe.wait_ge(dec_tanh, n + 1)
                for c, name in enumerate(("dec2a", "dec2b")):
                    nc.tensor.matmul(a_bank(n, name)[:, :], low_w[DEC:2 * DEC, P * c:P * c + P], low_t[DEC:2 * DEC, :],
                                     start=True, stop=True).then_inc(a_done, 1)

            def a_proj(n, j, letter, weight):
                pe.wait_ge(x5_ready, n * 5 + j + 1)
                for o in range(EC):
                    project(a_bank(n, f"{letter}{o}"), weight, x5_half(j), o).then_inc(a_done, 1)

            def b_head_sum(n, h):
                pe.wait_ge(ruk_ready, n * 2 + h + 1)
                wait(pe, bonus_ready, n * 2 + h)
                nc.tensor.matmul(sbank[:, :], ones_head, bon[h][:, :], start=True, stop=True).then_inc(head_sum, 1)

            def b_reduce(n, h, q):
                pe.wait_ge(prod_ready, n * 4 + 2 * h + q + 1)
                if q == 0:
                    wait(pe, gn_scaled, n * 2 + h - 1)
                for i in range(4):
                    mm = nc.tensor.matmul(att[h][:, :], cst[:, C_PROD + 4 * q + i, :], vb[h][:, 4 * q + i, :],
                                          start=(q == 0 and i == 0), stop=False)
                mm.then_inc(prod_used, 1)

            def b_bonus(n, h):
                pe.wait_ge(bonus_ready, n * 2 + h + 1)
                nc.tensor.matmul(att[h][:, :], cst[:, C_SELF, :], bon[h][:, :], start=False, stop=True).then_inc(att_done, 1)

            def c_var(n):
                for h in range(2):
                    pe.wait_ge(att_sq, n * 2 + h + 1)
                    nc.tensor.matmul(c_bank(n, f"var{h}")[:, :], avg_head, sq[h][:, :], start=True, stop=True).then_inc(c_done, 1)

            def rows(n, name, lhs, weight):
                i = int(name[1])
                bank = c_bank(n, name)
                for m in range(2):
                    for c in range(EC):
                        lo = P * (2 * i + m)
                        mm = nc.tensor.matmul(bank[:, E * m:E * m + E], lhs(c)[:, lo:lo + P], wsq[:, weight, c, :],
                                              start=(c == 0), stop=(c == EC - 1))
                mm.then_inc(c_done, 1)

            def c_out(n):
                pe.wait_ge(ag_ready, n * 2 + 2)
                rows(n, "o0", lambda c: ag[:, c, :], WO)
                rows(n, "o1", lambda c: ag[:, c, :], WO)

            def c_turn(n):
                pe.wait_ge(zn2_ready, n * TILES + TILES)
                for c in range(EC):
                    turn(zn2, c_bank, n, c).then_inc(c_done, 1)

            def c_key(n):
                pe.wait_ge(xk_ready, n * 2 + 2)
                for o in range(EC):
                    project(c_bank(n, f"k{o}"), FK, lambda c: zn2[:, TOK * c:TOK * c + TOK], o).then_inc(c_done, 1)

            def c_recept(n):
                pe.wait_ge(xr_ready, n * 2 + 2)
                rows(n, "r0", lambda c: xrr[:, c, :], FR)
                rows(n, "r1", lambda c: xrr[:, c, :], FR)

            def c_value(n):
                pe.wait_ge(kk_ready, n * 2 + 2)
                rows(n, "v0", lambda c: kk[:, c, :], FV)
                rows(n, "v1", lambda c: kk[:, c, :], FV)

            def body(n, a=True, b=True, c=True):
                if b:
                    a_proj(n, 4, "g", WG)
                if a:
                    a_turn(n + 1)
                if c:
                    c_var(n - 1)
                if b:
                    b_head_sum(n, 0)
                if a:
                    a_mix(n + 1)
                    a_mod(n + 1, 0)
                if c:
                    c_out(n - 1)
                if b:
                    b_head_sum(n, 1)
                if a:
                    a_mod(n + 1, 1)
                if b:
                    b_reduce(n, 0, 0)
                if a:
                    a_mod(n + 1, 2)
                    a_dec1(n + 1)
                if b:
                    b_reduce(n, 0, 1)
                if c:
                    c_turn(n - 1)
                if a:
                    a_dec2(n + 1)
                    a_proj(n + 1, 1, "v", WV)
                if c:
                    c_key(n - 1)
                if a:
                    a_mod(n + 1, 3)
                if c:
                    c_recept(n - 1)
                    c_value(n - 1)
                if a:
                    a_proj(n + 1, 2, "k", WK)
                    a_mod(n + 1, 4)
                if b:
                    b_reduce(n, 1, 0)
                if a:
                    a_proj(n + 1, 3, "r", WR)
                if b:
                    b_bonus(n, 0)
                    b_reduce(n, 1, 1)
                    b_bonus(n, 1)

            warm(WARM_D)
            a_turn(0)
            warm(9)
            a_mix(0)
            a_mod(0, 0)
            warm(2)
            a_mod(0, 1)
            warm(1)
            a_mod(0, 2)
            a_dec1(0)
            warm(2)
            a_dec2(0)
            a_proj(0, 1, "v", WV)
            a_mod(0, 3)
            a_proj(0, 2, "k", WK)
            a_mod(0, 4)
            a_proj(0, 3, "r", WR)
            a_proj(0, 4, "g", WG)
            b_head_sum(0, 0)
            a_turn(1)
            b_head_sum(0, 1)
            b_reduce(0, 0, 0)
            a_mix(1)
            a_mod(1, 0)
            a_mod(1, 1)
            a_mod(1, 2)
            a_dec1(1)
            b_reduce(0, 0, 1)
            a_dec2(1)
            a_proj(1, 1, "v", WV)
            a_mod(1, 3)
            b_bonus(0, 0)
            a_proj(1, 2, "k", WK)
            a_mod(1, 4)
            a_proj(1, 3, "r", WR)
            b_reduce(0, 1, 0)
            b_reduce(0, 1, 1)
            b_bonus(0, 1)
            with pe.Fori(1, CHUNKS - 2, 2) as n:
                body(n)
                body(n + 1)
            c_var(CHUNKS - 2)
            a_proj(CHUNKS - 1, 4, "g", WG)
            b_head_sum(CHUNKS - 1, 0)
            c_out(CHUNKS - 2)
            b_reduce(CHUNKS - 1, 0, 0)
            b_head_sum(CHUNKS - 1, 1)
            b_reduce(CHUNKS - 1, 0, 1)
            b_bonus(CHUNKS - 1, 0)
            c_turn(CHUNKS - 2)
            b_reduce(CHUNKS - 1, 1, 0)
            c_key(CHUNKS - 2)
            c_recept(CHUNKS - 2)
            c_value(CHUNKS - 2)
            b_reduce(CHUNKS - 1, 1, 1)
            b_bonus(CHUNKS - 1, 1)
            c_var(CHUNKS - 1)
            warm(12)
            c_out(CHUNKS - 1)
            warm(11)
            c_turn(CHUNKS - 1)
            warm(8)
            c_key(CHUNKS - 1)
            c_recept(CHUNKS - 1)
            c_value(CHUNKS - 1)

        @block.scalar
        def _(act):
            def a_bias(n):
                act.wait_ge(x_in, n * 16 + 16)
                nc.scalar.activation(xr_in[:, :, :], xr_in[:, :, :], ACT.Identity, bias=t["bnb"][:, 0:1]).then_inc(x_biased, 1)

            def a_xn(n):
                wait(act, x5_ready, n * 5)
                for c in range(EC):
                    act.wait_ge(a_done, a_at(n, f"T{c}"))
                    nc.scalar.activation(xn[:, NB * c:NB * c + NB, 1:L1], bt(ab(f"T{c}")[:, :]), ACT.Identity,
                                         bias=col(LN1B, c), scale=col(LN1W, c)).then_inc(xn_ready, 1)

            def a_tanh(n):
                act.wait_ge(a_done, a_at(n, "m0"))
                nc.scalar.activation(t1[:, :], ab("m0")[:, :], ACT.Tanh).then_inc(mix_tanh, 1)
                act.wait_ge(a_done, a_at(n, "m1"))
                nc.scalar.activation(low_t[0:MIX, :], ab("m1")[0:MIX, :], ACT.Tanh).then_inc(mix_tanh, 1)

            def a_dec(n):
                act.wait_ge(a_done, a_at(n, "dec1"))
                nc.scalar.activation(low_t[DEC:2 * DEC, :], ab("dec1")[DEC:2 * DEC, :], ACT.Tanh).then_inc(dec_tanh, 1)

            def a_w(n, p):
                for h, name in enumerate(("dec2a", "dec2b")):
                    act.wait_ge(a_done, a_at(n, name))
                    nc.scalar.activation(w[p][h][:, :, 1:L1], bt(ab(name)[:, :]), ACT.Exp, bias=col(TDEC, h)).then_inc(dec_exp, 1)
                for h in range(2):
                    act.wait_ge(dec_exp, n * 2 + h + 1)
                    nc.scalar.activation(w[p][h][:, :, 1:L1], w[p][h][:, :, 1:L1], ACT.Exp, scale=-1.0).then_inc(w_ready, 1)

            def a_copy(n, letter, dst, sem_out):
                for h in range(2):
                    act.wait_ge(a_done, a_at(n, f"{letter}{h}"))
                    if letter == "v":
                        wait(act, bonus_ready, (n - 1) * 2 + h + 1)
                        wait(act, v_spread[h], n * 16 * S)
                    nc.scalar.activation(dst[h][:, :], ab(f"{letter}{h}")[:, :], ACT.Copy).then_inc(sem_out, 1)

            def a_gate(n, p):
                for h in range(2):
                    act.wait_ge(a_done, a_at(n, f"g{h}"))
                    nc.scalar.activation(gate[p][h][:, :], ab(f"g{h}")[:, :], ACT.Tanh, scale=0.5).then_inc(g_tanh, 1)

            def c_square(n):
                for h in range(2):
                    act.wait_ge(att_done, n * 2 + h + 1)
                    nc.scalar.activation(sq[h][:, :], att[h][:, :], ACT.Square).then_inc(att_sq, 1)

            def c_rstd(n):
                for h in range(2):
                    act.wait_ge(c_done, c_at(n, f"var{h}"))
                    nc.scalar.activation(sq[h][:, :], cb(f"var{h}")[:, :], ACT.Ln, bias=eps[:, 0:1]).then_inc(var_ln, 1)
                for h in range(2):
                    act.wait_ge(var_ln, n * 2 + h + 1)
                    nc.scalar.activation(sq[h][:, :], sq[h][:, :], ACT.Exp, scale=-0.5).then_inc(gn_rstd, 1)

            def c_xn2(n):
                for c in range(EC):
                    act.wait_ge(c_done, c_at(n, f"T{c}"))
                    nc.scalar.activation(xn2[:, NB * c:NB * c + NB, 1:L1], bt(cb(f"T{c}")[:, :]), ACT.Identity,
                                         bias=col(LN2B, c), scale=col(LN2W, c)).then_inc(xn2_ready, 1)

            def c_kk(n):
                for c in range(EC):
                    act.wait_ge(c_done, c_at(n, f"k{c}"))
                    nc.scalar.activation(kk[:, c, :], cb(f"k{c}")[:, :], ACT.Relu).then_inc(relu_ready, 1)
                for c in range(EC):
                    act.wait_ge(relu_ready, n * 2 + c + 1)
                    nc.scalar.activation(kk[:, c, :], kk[:, c, :], ACT.Square).then_inc(kk_ready, 1)

            def c_rr(n):
                for i in range(2):
                    act.wait_ge(c_done, c_at(n, f"r{i}"))
                    nc.scalar.activation(rr[:, 2 * i:2 * i + 2, :], cb(f"r{i}")[:, :].rearrange("p (m f) -> p m f", m=2),
                                         ACT.Tanh, scale=0.5).then_inc(rr_ready, 1)

            def body(n, p, a=True, b=True, c=True):
                q = 1 - p
                if a:
                    a_bias(n + 1)
                if c:
                    c_square(n - 1)
                if b:
                    a_gate(n, p)
                if a:
                    a_xn(n + 1)
                if c:
                    c_rstd(n - 1)
                if a:
                    a_tanh(n + 1)
                    a_dec(n + 1)
                if c:
                    c_xn2(n - 1)
                if a:
                    a_w(n + 1, q)
                    a_copy(n + 1, "v", v, v_ready)
                if c:
                    c_kk(n - 1)
                    c_rr(n - 1)
                if a:
                    a_copy(n + 1, "k", k[q], k_ready)
                    a_copy(n + 1, "r", r[q], r_ready)

            act.wait_ge(init_done, 5)
            a_bias(0)
            a_xn(0)
            a_bias(1)
            a_tanh(0)
            a_dec(0)
            a_w(0, 0)
            a_copy(0, "v", v, v_ready)
            a_copy(0, "k", k[0], k_ready)
            a_copy(0, "r", r[0], r_ready)
            a_gate(0, 0)
            a_xn(1)
            a_tanh(1)
            a_dec(1)
            a_w(1, 1)
            a_copy(1, "v", v, v_ready)
            a_copy(1, "k", k[1], k_ready)
            a_copy(1, "r", r[1], r_ready)
            with act.Fori(1, CHUNKS - 2, 2) as n:
                body(n, 1)
                body(n + 1, 0)
            c_square(CHUNKS - 2)
            c_rstd(CHUNKS - 2)
            a_gate(CHUNKS - 1, 1)
            c_xn2(CHUNKS - 2)
            c_kk(CHUNKS - 2)
            c_rr(CHUNKS - 2)
            body(CHUNKS, CHUNKS % 2, a=False, b=False)

        @block.vector
        def _(dve):
            def moments(n, src_sem, src_at, stb, mvb, veb, s_st, s_mv, s_var):
                wait_apart(nc, dve, src_sem, src_at, eps[:, 1:2])
                for m in range(TILES):
                    nc.vector.bn_stats(stb[:, m, :], wyz[:, bass.ds(n * TILES + m, 1), :].rearrange("p a f -> p (a f)")).then_inc(s_st, 1)
                wait_apart(nc, dve, s_st, n * TILES + TILES, eps[:, 1:2])
                for m in range(TILES):
                    nc.vector.bn_aggr(mvb[:, m, :], stb[:, m, :]).then_inc(s_mv, 1)
                dve.wait_ge(s_mv, n * TILES + TILES)
                nc.vector.tensor_scalar(veb[:, :], mvb[:, :, 1], EPS, None, ALU.add).then_inc(s_var, 1)

            def normalise(n, s_rstd, mvb, rsb, dst, s_out):
                dve.wait_ge(s_rstd, n + 1)
                for m in range(TILES):
                    nc.vector.tensor_scalar(dst[:, E * m:E * m + E], wyz[:, bass.ds(n * TILES + m, 1), :].rearrange("p a f -> p (a f)"),
                                            mvb[:, m, 0:1], rsb[:, m:m + 1], ALU.subtract, ALU.mult).then_inc(s_out, 1)

            def a_z(n):
                dve.wait_ge(x_biased, n + 1)
                z = wyz[:, bass.ds(n * TILES, TILES), :]
                nc.vector.scalar_tensor_tensor(z, z, t["bna"][:, 0:1], xr_in[:, :, :], ALU.mult, ALU.add).then_inc(z_ready, 1)
                moments(n, z_ready, n + 1, st1b, mv1, ve1, st1, mv1_s, ln1_var)

            def a_norm(n):
                normalise(n, ln1_rstd, mv1, rs1, zn, zn_ready)

            def a_shift(n):
                dve.wait_ge(xn_ready, n * 2 + 2)
                dve.wait_ge(xprev, n * 2 + 2)
                nc.vector.tensor_tensor(sx[:, :, :], xn[:, :, 0:L], xn[:, :, 1:L1], ALU.subtract).then_inc(sx_ready, 1)
                dve.wait_ge(sx_ready, n + 1)
                for c in range(EC):
                    nc.vector.scalar_tensor_tensor(bt(xm[:, TOK * c:TOK * c + TOK]), sx[:, NB * c:NB * c + NB, :], col(MAAX, c),
                                                   xn[:, NB * c:NB * c + NB, 1:L1], ALU.mult, ALU.add).then_inc(xm_ready, 1)

            def a_mod(n, j):
                wait(dve, a_done, a_at(n, X5_READ_BY[j - 2]) if j >= 2 else a_at(n - 1, X5_READ_BY[4 - j]))
                for c, name in enumerate((f"w{j}a", f"w{j}b")):
                    dve.wait_ge(a_done, a_at(n, name))
                    nc.vector.scalar_tensor_tensor(x5[j % 2][:, NB * c:NB * c + NB, :], bt(ab(name)[:, :]), col(STK0 + MIX_OF[j], c),
                                                   sx[:, NB * c:NB * c + NB, :], ALU.add, ALU.mult).then_inc(mod_ready, 1)

            def a_gate(n, p):
                for h in range(2):
                    dve.wait_ge(g_tanh, n * 2 + h + 1)
                    nc.vector.scalar_tensor_tensor(gate[p][h][:, :], gate[p][h][:, :], 1.0, ab(f"g{h}")[:, :],
                                                   ALU.add, ALU.mult).then_inc(gate_ready, 1)

            def b_ruk(n, p):
                for h in range(2):
                    dve.wait_ge(k_ready, n * 2 + h + 1)
                    dve.wait_ge(r_ready, n * 2 + h + 1)
                    wait(dve, att_done, n * 2 + h - 1)
                    nc.vector.scalar_tensor_tensor(bon[h][:, :], r[p][h][:, :], col(BONUS, h), k[p][h][:, :], ALU.mult, ALU.mult).then_inc(ruk_ready, 1)

            def b_bonus(n, h):
                dve.wait_ge(head_sum, n * 2 + h + 1)
                dve.wait_ge(v_ready, n * 2 + h + 1)
                nc.vector.tensor_tensor(bon[h][:, :], sbank[:, :], v[h][:, :], ALU.mult).then_inc(bonus_ready, 1)

            def wide(ap):
                return bt(ap).rearrange("p b (a t) -> p a b t", a=1).broadcast_to([P, 4, NB, L])

            def b_kv(n, p, h, q):
                if q == 0:
                    dve.wait_ge(v_spread[h], n * 16 * S + 16 * S)
                    dve.wait_ge(k_ready, n * 2 + h + 1)
                part = 2 * h + q
                src = vb[h][:, 4 * q:4 * q + 4, :].rearrange("p e (b t) -> p e b t", t=L)
                wait(dve, prod_ready, n * 4 + part)
                nc.vector.tensor_tensor(st[:, :, :, 1:L1], src, wide(k[p][h][:, :]), ALU.mult).then_inc(kv_ready, 1)
                nc.vector.tensor_copy(st[:, :, :, 0], t["s0"][:, h, 4 * q:4 * q + 4, bass.ds(n * NB, NB)]).then_inc(kv_ready, 1)

            def b_scan(n, p, h, q):
                part = 2 * h + q
                src = vb[h][:, 4 * q:4 * q + 4, :].rearrange("p e (b t) -> p e b t", t=L)
                if q == 0:
                    dve.wait_ge(w_ready, n * 2 + h + 1)
                dve.wait_ge(kv_ready, n * 8 + 2 * part + 2)
                for i in range(4):
                    row = st[:, i, :, :].rearrange("p b t -> p (b t)")
                    nc.vector.tensor_tensor_scan(row, w[p][h][:, :, :].rearrange("p b t -> p (b t)"), row, 0.0,
                                                 ALU.mult, ALU.add).then_inc(scanned, 1)
                if q == 0:
                    dve.wait_ge(r_ready, n * 2 + h + 1)
                dve.wait_ge(scanned, n * 16 + 4 * part + 4)
                nc.vector.tensor_tensor(src, st[:, :, :, 0:L], wide(r[p][h][:, :]), ALU.mult).then_inc(prod_ready, 1)

            def c_gn(n, p):
                for h in range(2):
                    dve.wait_ge(gn_rstd, n * 2 + h + 1)
                    nc.vector.scalar_tensor_tensor(ag[:, h, :], att[h][:, :], col(GNW, h), sq[h][:, :], ALU.mult, ALU.mult).then_inc(gn_scaled, 1)
                for h in range(2):
                    dve.wait_ge(gn_scaled, n * 2 + h + 1)
                    dve.wait_ge(gate_ready, n * 2 + h + 1)
                    nc.vector.scalar_tensor_tensor(ag[:, h, :], ag[:, h, :], col(GNB, h), gate[p][h][:, :], ALU.add, ALU.mult).then_inc(ag_ready, 1)

            def c_x1(n):
                for i in range(2):
                    dve.wait_ge(c_done, c_at(n, f"o{i}"))
                    z = wyz[:, bass.ds(n * TILES + 2 * i, 2), :]
                    nc.vector.scalar_tensor_tensor(z, cb(f"o{i}")[:, :].rearrange("p (m f) -> p m f", m=2), 0.5, z,
                                                   ALU.mult, ALU.add).then_inc(x1_ready, 1)
                moments(n, x1_ready, n * 2 + 2, st2b, mv2, ve2, st2, mv2_s, ln2_var)

            def c_norm(n):
                normalise(n, ln2_rstd, mv2, rs2, zn2, zn2_ready)

            def c_shift(n):
                dve.wait_ge(xn2_ready, n * 2 + 2)
                dve.wait_ge(xprev2, n * 2 + 2)
                dve.wait_ge(stored, n * 16 + 16)
                nc.vector.tensor_tensor(sx2[:, :, :], xn2[:, :, 0:L], xn2[:, :, 1:L1], ALU.subtract).then_inc(sx2_ready, 1)
                dve.wait_ge(sx2_ready, n + 1)
                for dst, v_, s_out in ((lambda c: zn2[:, TOK * c:TOK * c + TOK], FMK, xk_ready), (lambda c: xrr[:, c, :], FMR, xr_ready)):
                    for c in range(EC):
                        nc.vector.scalar_tensor_tensor(bt(dst(c)), sx2[:, NB * c:NB * c + NB, :], col(v_, c),
                                                       xn2[:, NB * c:NB * c + NB, 1:L1], ALU.mult, ALU.add).then_inc(s_out, 1)

            def c_final(n):
                for i in range(2):
                    dve.wait_ge(rr_ready, n * 2 + i + 1)
                    dve.wait_ge(c_done, c_at(n, f"v{i}"))
                    if i == 0:
                        dve.wait_ge(xr_ready, n * 2 + 2)
                    nc.vector.scalar_tensor_tensor(y[:, 2 * i:2 * i + 2, :], rr[:, 2 * i:2 * i + 2, :], 1.0,
                                                   cb(f"v{i}")[:, :].rearrange("p (m f) -> p m f", m=2), ALU.add, ALU.mult).then_inc(y_mid, 1)
                for i in range(2):
                    dve.wait_ge(y_mid, n * 2 + i + 3)
                    nc.vector.scalar_tensor_tensor(y[:, 2 * i:2 * i + 2, :], y[:, 2 * i:2 * i + 2, :], 0.5,
                                                   wyz[:, bass.ds(n * TILES + 2 * i, 2), :], ALU.mult, ALU.add).then_inc(out_ready, 1)

            def body(n, p, a=True, b=True, c=True):
                q = 1 - p
                if b:
                    b_kv(n, p, 0, 0)
                    b_scan(n, p, 0, 0)
                if a:
                    a_z(n + 1)
                if b:
                    b_ruk(n, p)
                if a:
                    a_norm(n + 1)
                if b:
                    a_gate(n, p)
                if a:
                    a_shift(n + 1)
                if b:
                    b_kv(n, p, 0, 1)
                if c:
                    c_gn(n - 1, q)
                if a:
                    a_mod(n + 1, 0)
                if b:
                    b_bonus(n, 0)
                    b_scan(n, p, 0, 1)
                if a:
                    a_mod(n + 1, 1)
                if c:
                    c_x1(n - 1)
                if b:
                    b_bonus(n, 1)
                if c:
                    c_norm(n - 1)
                if a:
                    a_mod(n + 1, 2)
                if b:
                    b_kv(n, p, 1, 0)
                if c:
                    c_shift(n - 1)
                if b:
                    b_scan(n, p, 1, 0)
                if a:
                    a_mod(n + 1, 3)
                if b:
                    b_kv(n, p, 1, 1)
                    b_scan(n, p, 1, 1)
                if c:
                    c_final(n - 1)
                if a:
                    a_mod(n + 1, 4)

            nc.vector.memset(eps[:, 0:1], EPS).then_inc(init_done, 1)
            for p in range(2):
                for h in range(2):
                    nc.vector.memset(w[p][h][:, :, 0], 0.0).then_inc(init_done, 1)
            dve.sem_inc(y_mid, 2)
            dve.sem_inc(stored, 16)
            dve.wait_ge(init_done, 5)
            a_z(0)
            a_norm(0)
            a_shift(0)
            a_z(1)
            a_mod(0, 0)
            a_mod(0, 1)
            a_mod(0, 2)
            a_norm(1)
            a_mod(0, 3)
            a_mod(0, 4)
            b_kv(0, 0, 0, 0)
            b_scan(0, 0, 0, 0)
            b_ruk(0, 0)
            a_gate(0, 0)
            b_bonus(0, 0)
            b_kv(0, 0, 0, 1)
            a_shift(1)
            b_scan(0, 0, 0, 1)
            a_mod(1, 0)
            a_mod(1, 1)
            b_kv(0, 0, 1, 0)
            a_mod(1, 2)
            b_scan(0, 0, 1, 0)
            b_bonus(0, 1)
            b_kv(0, 0, 1, 1)
            a_mod(1, 3)
            b_scan(0, 0, 1, 1)
            a_mod(1, 4)
            with dve.Fori(1, CHUNKS - 2, 2) as n:
                body(n, 1)
                body(n + 1, 0)
            b_kv(CHUNKS - 1, 1, 0, 0)
            b_scan(CHUNKS - 1, 1, 0, 0)
            b_kv(CHUNKS - 1, 1, 0, 1)
            b_scan(CHUNKS - 1, 1, 0, 1)
            b_ruk(CHUNKS - 1, 1)
            c_gn(CHUNKS - 2, 0)
            b_kv(CHUNKS - 1, 1, 1, 0)
            c_x1(CHUNKS - 2)
            b_bonus(CHUNKS - 1, 0)
            c_norm(CHUNKS - 2)
            b_scan(CHUNKS - 1, 1, 1, 0)
            c_shift(CHUNKS - 2)
            a_gate(CHUNKS - 1, 1)
            b_kv(CHUNKS - 1, 1, 1, 1)
            b_bonus(CHUNKS - 1, 1)
            b_scan(CHUNKS - 1, 1, 1, 1)
            c_final(CHUNKS - 2)
            body(CHUNKS, CHUNKS % 2, a=False, b=False)


def program(nc, d, out):
    ctx = ExitStack()
    with ctx:
        def sb(name, shape):
            return ctx.enter_context(nc.sbuf_tensor(name, shape, F32))

        def sem(name):
            return ctx.enter_context(nc.semaphore(name))

        t = {
            "wyz": sb("wyz", [P, PAIRS, T]),
            "stats": sb("stats", [P, PAIRS, 6]),
            "cst": sb("cst", [P, 13, P]),
            "vec": sb("vec", [P, 16, EC]),
            "bnv": sb("bnv", [P, 2]),
            "wsq": sb("wsq", [P, 8, EC, E]),
            "w1": sb("w1", [P, EC, 5 * MIX]),
            "w2": sb("w2", [P, E]),
            "low_w": sb("low_w", [P, E]),
            "dw1": sb("dw1", [P, EC, DEC]),
            "s0": sb("s0", [P, 2, S, B]),
            "prev1": sb("prev1", [P, EC, B]),
            "prev0": sb("prev0", [P, EC, B]),
            "bna": sb("bna", [P, 1]),
            "bnb": sb("bnb", [P, 1]),
            "mhalf": sb("mhalf", [P, TILES]),
            "s_late": sem("late_weights_in"),
            "x_chunk": sb("x_chunk", [P, TILES, E]),
            "x_in": sem("x_in"),
        }
        attention(nc, sem, t, d)
        norm_params(nc, sem, t)
        rwkv(nc, sem, t, d, out)


def _constants():
    import numpy as np

    i = np.arange(P)
    same_head = (i[:, None] // S == i[None, :] // S).astype(np.float32)
    out = np.zeros((13, P, P), np.float32)
    for e in range(S):
        out[C_PROD + e] = same_head * ((i[None, :] % S == e).astype(np.float32) - 1.0 / S)
    out[C_SELF] = np.eye(P, dtype=np.float32) - same_head / S
    out[C_ONES] = same_head
    out[C_AVG] = same_head / S
    out[C_HALF] = (i[:, None] % C == i[None, :] % C).astype(np.float32) * 0.5
    out[C_ID] = np.eye(P, dtype=np.float32)
    return np.ascontiguousarray(out.transpose(1, 0, 2))


def kernel(**inputs):
    import numpy as np
    import concourse.bacc as bacc
    from concourse.bass_utils import run_bass_kernel_spmd

    a = {k: np.asarray(v) for k, v in inputs.items()}
    p1 = {k[len("L1_xattn_"):]: v for k, v in a.items() if k.startswith("L1_xattn_")}
    p0 = {k[len("L0_xattn_"):]: v for k, v in a.items() if k.startswith("L0_xattn_")}
    ctx = a["ctx_2048"]

    def halves(m):
        return m.reshape(EC, P, -1).transpose(1, 0, 2)

    vecs = [p1["ln1_w"], p1["ln1_b"], p1["ln2_w"], p1["ln2_b"], p1["maa_x"], *p1["maa_stack"], p1["time_decay"],
            p1["faaaa"].reshape(-1), p1["gn_w"], p1["gn_b"], p1["ffn_maa_k"], p1["ffn_maa_r"]]
    squares = [p1[n] for n in ("Wr", "Wk", "Wv", "Wg", "Wo", "ffn_Wk", "ffn_Wr", "ffn_Wv")]
    arrays = {
        "x": a["x"].reshape(PAIRS, P, T),
        "ctx": ctx.reshape(PAIRS, P, T),
        "cst": _constants(),
        "Wg": p0["Wg"], "WzT": p0["Wz"].T, "WthT": p0["Wtheta"].T, "WphT": p0["Wphi"].T,
        "bg": p0["bg"].reshape(CI, 1), "bz": p0["bz"].reshape(1, C),
        "bth": np.concatenate([p0["btheta"]] * 2).reshape(2 * CI, 1),
        "bph": np.concatenate([p0["bphi"]] * 2).reshape(2 * CI, 1),
        "bnv": np.stack([np.concatenate([p0[n]] * 2) for n in ("gamma", "beta")], axis=1),
        "vec": halves(np.stack(vecs, axis=1)).transpose(0, 2, 1),
        "wsq": np.stack([halves(m.T) for m in squares], axis=1),
        "w1": halves(p1["maa_w1"]),
        "w2": p1["maa_w2"].reshape(5 * MIX, E),
        "dw1": halves(p1["decay_w1"]),
        "dw2": p1["decay_w2"],
        "s0": ctx[:, 2:2 + S, :].reshape(B, 2, P, S).transpose(2, 1, 3, 0),
        "prev1": halves(ctx[:, 1, :].T),
        "prev0": halves(ctx[:, 0, :].T),
    }
    nc = bacc.Bacc("TRN2", target_bir_lowering=False, num_devices=1)
    feeds, d = {}, {}
    for name, m in arrays.items():
        m = np.ascontiguousarray(m)
        feeds[f"in_{name}"] = m
        d[name] = nc.dram_tensor(f"in_{name}", m.shape, mybir.dt.from_np(m.dtype), kind="ExternalInput").ap()
    out = nc.dram_tensor("out_0", (PAIRS, P, T), F32, kind="ExternalOutput").ap()
    program(nc, d, out)
    res = run_bass_kernel_spmd(nc, [feeds], core_ids=[0])
    return res.results[0]["out_0"].reshape(B, C, T)
```
